# Optimizing a Trainium2 kernel written in Bass

```python
import numpy as np
import jax
import jax.numpy as jnp

def _softmax(x, axis=-1):
    return jax.nn.softmax(x, axis=axis)

def _gelu(x):
    return jax.nn.gelu(x, approximate=True)

def _silu(x):
    return jax.nn.silu(x)

def _sigmoid(x):
    return jax.nn.sigmoid(x)

def _layernorm(x, axis=-1, eps=1e-05):
    m = jnp.mean(x, axis=axis, keepdims=True)
    v = jnp.var(x, axis=axis, keepdims=True)
    return (x - m) / jnp.sqrt(v + eps)

def _scatter_add(tgt, idx, src, axis=0):
    return tgt.at[idx].add(src)

def _segment_sum(src, seg, n):
    return jax.ops.segment_sum(src, seg, n)
kernel_name = 'mk_prb_d2_jaxref_r4_748498'

def setup_inputs(seed: int=0):
    np.random.seed(seed)
    _w = jnp.asarray

    def _L0_attn_setup():
        import jax, jax.numpy as jnp
        import numpy as np
        DIM = 256
        NUM_HEADS = 16
        HEAD_DIM = DIM // NUM_HEADS

        def _rope_tables(seq_len, dim, dtype):
            inv_freq = 1.0 / 10000.0 ** (jnp.arange(0, dim, 2, dtype=jnp.float32) / dim)
            t = jnp.arange(seq_len, dtype=jnp.float32)
            freqs = jnp.outer(t, inv_freq)
            return (jnp.cos(freqs).astype(dtype), jnp.sin(freqs).astype(dtype))

        def _apply_rope(x, cos_emb, sin_emb):
            x1 = x[..., 0::2]
            x2 = x[..., 1::2]
            return jnp.concatenate((x1 * cos_emb - x2 * sin_emb, x1 * sin_emb + x2 * cos_emb), axis=-1)
        key = jax.random.key(seed)
        k_x, k_qkv, k_out, k_b = jax.random.split(key, 4)
        B, S, D = (2, 512, DIM)
        x = jax.random.normal(k_x, (B, S, D), dtype=jnp.float32)
        w_qkv = jax.random.normal(k_qkv, (3 * D, D), dtype=jnp.float32) * (1.0 / np.sqrt(D))
        w_out = jax.random.normal(k_out, (D, D), dtype=jnp.float32) * (1.0 / np.sqrt(D))
        b_out = jax.random.normal(k_b, (D,), dtype=jnp.float32) * 0.01
        return {'x': x, 'w_qkv': w_qkv, 'w_out': w_out, 'b_out': b_out}
    _L0_attn_in = _L0_attn_setup()

    def _L0_ffn_setup():
        import jax, jax.numpy as jnp
        import numpy as np
        DIM = 256

        def _reference_tuple_inner(x, W_r, W_k, W_v, mu_r, mu_k):
            B, T, C = x.shape
            x_prev = jnp.concatenate([jnp.zeros((B, 1, C), x.dtype), x[:, :-1, :]], axis=1)
            xr = mu_r * x + (1.0 - mu_r) * x_prev
            xk = mu_k * x + (1.0 - mu_k) * x_prev
            r = jax.nn.sigmoid(jnp.einsum('btc,dc->btd', xr, W_r))
            k = jnp.einsum('btc,dc->btd', xk, W_k)
            k_act = jnp.square(jax.nn.relu(k))
            out = r * jnp.einsum('btc,dc->btd', k_act, W_v)
            new_state = x[:, -1, :]
            return (out, new_state)
        key = jax.random.key(seed)
        ks = jax.random.split(key, 6)
        B, T, C = (8, 512, DIM)
        x = jax.random.normal(ks[0], (B, T, C), dtype=jnp.float32)
        s = 1.0 / np.sqrt(C)
        W_r = jax.random.uniform(ks[1], (C, C), jnp.float32, -s, s)
        W_k = jax.random.uniform(ks[2], (C, C), jnp.float32, -s, s)
        W_v = jax.random.uniform(ks[3], (C, C), jnp.float32, -s, s)
        mu_r = jax.random.uniform(ks[4], (C,), jnp.float32)
        mu_k = jax.random.uniform(ks[5], (C,), jnp.float32)
        return {'x': x, 'W_r': W_r, 'W_k': W_k, 'W_v': W_v, 'mu_r': mu_r, 'mu_k': mu_k}
    _L0_ffn_in = _L0_ffn_setup()

    def _L1_attn_setup():
        import jax, jax.numpy as jnp
        import numpy as np
        HIDDEN, HEADS, HDIM = (256, 8, 64)
        B, S = (4, 2048)
        LN_EPS = 1e-06
        key = jax.random.key(seed)
        ks = jax.random.split(key, 12)
        inner = HEADS * HDIM
        sd = HIDDEN ** (-0.5)
        return {'x': jax.random.normal(ks[0], (B, S, HIDDEN), jnp.float32), 'Wq': jax.random.normal(ks[1], (HIDDEN, inner), jnp.float32) * sd, 'bq': jnp.zeros((inner,), jnp.float32), 'Wk': jax.random.normal(ks[2], (HIDDEN, inner), jnp.float32) * sd, 'bk': jnp.zeros((inner,), jnp.float32), 'Wv': jax.random.normal(ks[3], (HIDDEN, inner), jnp.float32) * sd, 'bv': jnp.zeros((inner,), jnp.float32), 'Wo': jax.random.normal(ks[4], (inner, HIDDEN), jnp.float32) * inner ** (-0.5), 'bo': jnp.zeros((HIDDEN,), jnp.float32), 'alpha': jnp.ones((HEADS, HDIM), jnp.float32), 'aug_param': jax.random.normal(ks[5], (1, HEADS, HDIM), jnp.float32), 'ln_scale': jnp.ones((HIDDEN,), jnp.float32), 'ln_bias': jnp.zeros((HIDDEN,), jnp.float32)}
    _L1_attn_in = _L1_attn_setup()

    def _L1_ffn_setup():
        import jax, jax.numpy as jnp
        import numpy as np
        D_MODEL = 256
        key = jax.random.key(seed)
        k_x, k_w, k_a1, k_a2 = jax.random.split(key, 4)
        x = jax.random.normal(k_x, (4, 512, D_MODEL), dtype=jnp.float32)
        weight = jax.random.normal(k_w, (D_MODEL, D_MODEL), dtype=jnp.float32) * 0.02
        aux_weight1 = jax.random.normal(k_a1, (D_MODEL, D_MODEL), dtype=jnp.float32) * 0.02
        aux_weight2 = jax.random.normal(k_a2, (D_MODEL, D_MODEL), dtype=jnp.float32) * 0.02
        bias = jnp.zeros((D_MODEL,), dtype=jnp.float32)
        return {'x': x, 'weight': weight, 'aux_weight1': aux_weight1, 'aux_weight2': aux_weight2, 'bias': bias}
    _L1_ffn_in = _L1_ffn_setup()
    _d = {'L0_attn_x': _L0_attn_in['x'], 'L0_attn_w_qkv': _L0_attn_in['w_qkv'], 'L0_attn_w_out': _L0_attn_in['w_out'], 'L0_attn_b_out': _L0_attn_in['b_out'], 'L0_ffn_W_r': _L0_ffn_in['W_r'], 'L0_ffn_W_k': _L0_ffn_in['W_k'], 'L0_ffn_W_v': _L0_ffn_in['W_v'], 'L0_ffn_mu_r': _L0_ffn_in['mu_r'], 'L0_ffn_mu_k': _L0_ffn_in['mu_k'], 'L1_attn_Wq': _L1_attn_in['Wq'], 'L1_attn_bq': _L1_attn_in['bq'], 'L1_attn_Wk': _L1_attn_in['Wk'], 'L1_attn_bk': _L1_attn_in['bk'], 'L1_attn_Wv': _L1_attn_in['Wv'], 'L1_attn_bv': _L1_attn_in['bv'], 'L1_attn_Wo': _L1_attn_in['Wo'], 'L1_attn_bo': _L1_attn_in['bo'], 'L1_attn_alpha': _L1_attn_in['alpha'], 'L1_attn_aug_param': _L1_attn_in['aug_param'], 'L1_attn_ln_scale': _L1_attn_in['ln_scale'], 'L1_attn_ln_bias': _L1_attn_in['ln_bias'], 'L1_ffn_weight': _L1_ffn_in['weight'], 'L1_ffn_aux_weight1': _L1_ffn_in['aux_weight1'], 'L1_ffn_aux_weight2': _L1_ffn_in['aux_weight2'], 'L1_ffn_bias': _L1_ffn_in['bias']}
    _x0 = _d['L0_attn_x']
    _d['L0_attn_x'] = jax.random.normal(jax.random.fold_in(jax.random.key(seed), 1), (4, 2048, 256), dtype=_x0.dtype)
    del _x0
    return _d

def reference(L0_attn_x, L0_attn_w_qkv, L0_attn_w_out, L0_attn_b_out, L0_ffn_W_r, L0_ffn_W_k, L0_ffn_W_v, L0_ffn_mu_r, L0_ffn_mu_k, L1_attn_Wq, L1_attn_bq, L1_attn_Wk, L1_attn_bk, L1_attn_Wv, L1_attn_bv, L1_attn_Wo, L1_attn_bo, L1_attn_alpha, L1_attn_aug_param, L1_attn_ln_scale, L1_attn_ln_bias, L1_ffn_weight, L1_ffn_aux_weight1, L1_ffn_aux_weight2, L1_ffn_bias):

    def _L0_attn_ref(x, w_qkv, w_out, b_out):
        import jax, jax.numpy as jnp
        import numpy as np
        DIM = 256
        NUM_HEADS = 16
        HEAD_DIM = DIM // NUM_HEADS

        def _rope_tables(seq_len, dim, dtype):
            inv_freq = 1.0 / 10000.0 ** (jnp.arange(0, dim, 2, dtype=jnp.float32) / dim)
            t = jnp.arange(seq_len, dtype=jnp.float32)
            freqs = jnp.outer(t, inv_freq)
            return (jnp.cos(freqs).astype(dtype), jnp.sin(freqs).astype(dtype))

        def _apply_rope(x, cos_emb, sin_emb):
            x1 = x[..., 0::2]
            x2 = x[..., 1::2]
            return jnp.concatenate((x1 * cos_emb - x2 * sin_emb, x1 * sin_emb + x2 * cos_emb), axis=-1)
        B, S, D = x.shape
        H, hd = (NUM_HEADS, HEAD_DIM)
        qkv = jnp.einsum('bsd,ed->bse', x, w_qkv)
        q, k, v = jnp.split(qkv, 3, axis=-1)
        q, k, v = (t.reshape(B, S, H, hd).transpose(0, 2, 1, 3) for t in (q, k, v))
        cos_emb, sin_emb = _rope_tables(S, hd, x.dtype)
        q = _apply_rope(q, cos_emb, sin_emb)
        k = _apply_rope(k, cos_emb, sin_emb)
        scores = jnp.einsum('bhqd,bhkd->bhqk', q, k) / jnp.sqrt(jnp.asarray(hd, x.dtype))
        attn = jax.nn.softmax(scores, axis=-1)
        out = jnp.einsum('bhqk,bhkd->bhqd', attn, v)
        out = out.transpose(0, 2, 1, 3).reshape(B, S, D)
        return jnp.einsum('bsd,ed->bse', out, w_out) + b_out

    def _L0_ffn_ref(x, W_r, W_k, W_v, mu_r, mu_k):
        import jax, jax.numpy as jnp
        import numpy as np
        DIM = 256

        def _reference_tuple_inner(x, W_r, W_k, W_v, mu_r, mu_k):
            B, T, C = x.shape
            x_prev = jnp.concatenate([jnp.zeros((B, 1, C), x.dtype), x[:, :-1, :]], axis=1)
            xr = mu_r * x + (1.0 - mu_r) * x_prev
            xk = mu_k * x + (1.0 - mu_k) * x_prev
            r = jax.nn.sigmoid(jnp.einsum('btc,dc->btd', xr, W_r))
            k = jnp.einsum('btc,dc->btd', xk, W_k)
            k_act = jnp.square(jax.nn.relu(k))
            out = r * jnp.einsum('btc,dc->btd', k_act, W_v)
            new_state = x[:, -1, :]
            return (out, new_state)
        return _reference_tuple_inner(x, W_r, W_k, W_v, mu_r, mu_k)[0]

    def _L1_attn_ref(x, Wq, bq, Wk, bk, Wv, bv, Wo, bo, alpha, aug_param, ln_scale, ln_bias):
        import jax, jax.numpy as jnp
        import numpy as np
        HIDDEN, HEADS, HDIM = (256, 8, 64)
        B, S = (4, 2048)
        LN_EPS = 1e-06
        b, s, _ = x.shape
        h, d = alpha.shape
        scale = d ** (-0.5)
        q = (x @ Wq + bq).reshape(b, s, h, d)
        k = (x @ Wk + bk).reshape(b, s, h, d)
        v = (x @ Wv + bv).reshape(b, s, h, d)
        decay = jax.nn.sigmoid(alpha)

        def step(state, qkv):
            q_t, k_t, v_t = qkv
            attn = jax.nn.softmax(jnp.einsum('bhd,bhd->bh', q_t, k_t) * scale, axis=-1)
            new_state = decay * state + (1.0 - decay) * attn[..., None] * v_t
            return (new_state, new_state)
        qs = jnp.moveaxis(q, 1, 0)
        ks_ = jnp.moveaxis(k, 1, 0)
        vs = jnp.moveaxis(v, 1, 0)
        init = jnp.zeros((b, h, d), x.dtype)
        _, states = jax.lax.scan(step, init, (qs, ks_, vs))
        states = jnp.moveaxis(states, 0, 1)
        aug = jax.nn.sigmoid(q * aug_param)
        out = (q * states + aug).reshape(b, s, h * d)
        out = out @ Wo + bo
        mean = jnp.mean(out, axis=-1, keepdims=True)
        var = jnp.var(out, axis=-1, keepdims=True)
        return (out - mean) * jax.lax.rsqrt(var + LN_EPS) * ln_scale + ln_bias

    def _L1_ffn_ref(x, weight, aux_weight1, aux_weight2, bias):
        import jax, jax.numpy as jnp
        import numpy as np
        D_MODEL = 256
        h = jnp.einsum('btc,cd->btd', x, weight)
        h = jnp.einsum('btc,cd->btd', h, aux_weight1)
        h = jnp.einsum('btc,cd->btd', h, aux_weight2)
        return jnp.tanh(h + bias)
    x = L0_attn_x
    xn = _layernorm(x, axis=-1)
    x = x + _L0_attn_ref(xn, L0_attn_w_qkv, L0_attn_w_out, L0_attn_b_out) + _L0_ffn_ref(xn, L0_ffn_W_r, L0_ffn_W_k, L0_ffn_W_v, L0_ffn_mu_r, L0_ffn_mu_k)
    xn = _layernorm(x, axis=-1)
    x = x + _L1_attn_ref(xn, L1_attn_Wq, L1_attn_bq, L1_attn_Wk, L1_attn_bk, L1_attn_Wv, L1_attn_bv, L1_attn_Wo, L1_attn_bo, L1_attn_alpha, L1_attn_aug_param, L1_attn_ln_scale, L1_attn_ln_bias) + _L1_ffn_ref(xn, L1_ffn_weight, L1_ffn_aux_weight1, L1_ffn_aux_weight2, L1_ffn_bias)
    return x

_drawn_inputs = setup_inputs


def setup_inputs(seed=0):
    import zlib

    import numpy as np

    out = dict(_drawn_inputs(seed))
    spreads = {'L1_attn_bq': (0.0, 0.288),
     'L1_attn_bk': (0.0, 0.8),
     'L1_attn_bv': (0.0, 0.485),
     'L1_attn_bo': (0.0, 0.1),
     'L1_attn_alpha': (1.0, 0.6),
     'L1_attn_ln_scale': (1.0, 0.2),
     'L1_attn_ln_bias': (0.0, 0.1),
     'L1_ffn_bias': (0.0, 0.1)}
    factors = {'L0_attn_b_out': 8.0, 'L0_ffn_W_r': 4.304, 'L0_ffn_mu_r': 8.0}
    for name, (base, spread) in spreads.items():
        noise = np.random.default_rng([zlib.crc32(name.encode()), seed]).standard_normal(out[name].shape)
        drawn = base * np.exp(spread * noise) if base else spread * noise
        out[name] = jnp.asarray(drawn.astype(out[name].dtype))
    for name, factor in factors.items():
        out[name] = (out[name] * factor).astype(out[name].dtype)
    return out
```

```python
import numpy as np
from contextlib import ExitStack

import concourse.bass as bass
from concourse import mybir

F32 = mybir.dt.float32
BF16 = mybir.dt.bfloat16
I32 = mybir.dt.int32
ALU = mybir.AluOpType
ACT = mybir.ActivationFunctionType
AX = mybir.AxisListType

P = 128
B, S, D = 4, 2048, 256
H, HD = 16, 16
NG = B * H
CH = 512
NC = S // CH
TT = CH // P
KT = S // P
DT = D // P
INNER = 512
H2, HD2 = 8, 64
IT = INNER // P
EPS1, EPS2 = 1e-5, 1e-6
NPARTS = 3
ROWS = 6 * HD
NBANK = 8
RSQRT_SEED = 0x5F3759DF


def build(nc, a, out):
    scratch_q = nc.dram_tensor("scratch_q", [NPARTS, B * D, S], BF16, kind="Internal").ap()
    scratch_k = nc.dram_tensor("scratch_k", [NPARTS, B * D, S], BF16, kind="Internal").ap()
    scratch_x = nc.dram_tensor("scratch_x", [B * S, D], F32, kind="Internal").ap()
    scratch_o = nc.dram_tensor("scratch_o", [NG * 32, S], F32, kind="Internal").ap()

    x_rows = a["x"].rearrange("b s d -> (b s) d")
    out_rows = out.rearrange("b s d -> (b s) d")

    top = ExitStack()
    with top:
        def sem(name):
            return top.enter_context(nc.semaphore(name))

        def sems(name, n):
            return [sem(f"{name}{i}") for i in range(n)]

        def allocator(stack):
            def sb(name, shape, dt=F32):
                return stack.enter_context(nc.sbuf_tensor(name, shape, dt))
            return sb

        ident = allocator(top)("ident", [P, P])
        psum = top.enter_context(nc.psum_tensor("psum", [P, NBANK, 512], F32))

        first = ExitStack()
        sb = allocator(first)
        v_all = sb("v_all", [P, NG, KT, HD])
        keep = ExitStack()
        sb = allocator(keep)
        w_qk = sb("w_qk", [P, DT, 2 * D])
        w_v = sb("w_v", [P, DT, D])
        wf_r = sb("wf_r", [P, DT, D])
        wf_k = sb("wf_k", [P, DT, D])
        wf_v = sb("wf_v", [P, DT, D])
        mu = sb("mu", [P, 2, DT])
        b_out = sb("b_out", [P, D])
        cos_t = sb("cos_t", [P, S])
        sin_t = sb("sin_t", [P, S])
        x_in = [sb(f"x_in{p}", [P, TT, D]) for p in range(2)]
        xn = [sb(f"xn{p}", [P, TT, D]) for p in range(2)]
        xn_t = [sb(f"xn_t{p}", [P, DT, CH + 1]) for p in range(2)]
        x_mix = [sb(f"x_mix{p}", [P, 2, DT, CH]) for p in range(2)]
        x_dif = sb("x_dif", [P, DT, CH])
        r_cos = [sb(f"r_cos{j}", [P, CH]) for j in range(4)]
        r_sin = [sb(f"r_sin{j}", [P, CH]) for j in range(4)]
        parts = [sb(f"parts{j}", [P, NPARTS, CH], BF16) for j in range(4)]
        r_gate = [sb(f"r_gate{i}", [P, 512]) for i in range(2)]
        k_act = sb("k_act", [P, DT, CH])
        stats1 = sb("stats1", [P, TT, 6])
        mv1 = sb("mv1", [P, TT, 2])
        nt1 = sb("nt1", [P, 4, TT])
        keep.close()

        attn = ExitStack()
        sb = allocator(attn)
        NSTK, NP = 3, 4
        q_stk = [sb(f"q_stk{j}", [P, S], BF16) for j in range(NSTK)]
        k_stk = [sb(f"k_stk{j}", [P, S], BF16) for j in range(NSTK)]
        v_head = [sb(f"v_head{j}", [P, KT, 2 * HD]) for j in range(NSTK)]
        probs = [sb(f"probs{n}", [P, S]) for n in range(NP)]
        o_head = [sb(f"o_head{j}", [P, 512]) for j in range(NSTK)]
        max_part = [sb(f"max_part{i}", [P, KT, 4]) for i in range(NSTK)]
        neg_max = sb("neg_max", [P, KT])
        neg_hl = sb("neg_hl", [P, 2, KT], BF16)
        neg_t = [sb(f"neg_t{j}", [P, 32], BF16) for j in range(NSTK)]
        attn.close()
        first.close()

        second = ExitStack()
        sb = allocator(second)
        w_out = sb("w_out", [P, DT, D])
        w2 = {n: sb(f"w2{n}", [P, DT, INNER]) for n in "qkv"}
        w_o2 = sb("w_o2", [P, IT, D])
        wa = {n: sb(f"wa_{n}", [P, DT, D]) for n in ("w", "1", "2")}
        w_12 = sb("w_12", [P, DT, D])
        w_ffn = sb("w_ffn", [P, DT, D])
        col = sb("col", [P, 5, IT])
        half_aug = sb("half_aug", [P, IT])
        decay = sb("decay", [P, IT])
        v_scale = sb("v_scale", [P, IT])
        v_bias = sb("v_bias", [P, IT])
        row_bc = sb("row_bc", [P, 4, D])
        head_sel = sb("head_sel", [P, 32])
        xc = [sb(f"xc{c}", [P, TT, D]) for c in range(NC)]
        a_raw = [sb(f"a_raw{p}", [P, DT, CH]) for p in range(2)]
        a_sum = [sb(f"a_sum{p}", [P, DT, CH]) for p in range(2)]
        xn2 = sb("xn2", [P, TT, D])
        xn2_t = [sb(f"xn2_t{p}", [P, DT, CH]) for p in range(2)]
        q2 = sb("q2", [P, IT, CH])
        qk2 = sb("qk2", [P, IT, CH])
        v2 = sb("v2", [P, IT, CH])
        state = [sb(f"state{p}", [P, IT, CH]) for p in range(2)]
        gate2 = sb("gate2", [P, IT, CH])
        o2 = sb("o2", [P, IT, CH])
        lg = sb("lg", [P, CH])
        aw = sb("aw", [P, TT, H2])
        aw_wide = sb("aw_wide", [P, TT, INNER])
        aw_small = sb("aw_small", [P, 3, TT])
        z2 = sb("z2", [P, TT, D])
        f2 = sb("f2", [P, TT, D])
        stats2 = sb("stats2", [P, TT, 6])
        mv2 = sb("mv2", [P, TT, 2])
        nt2 = sb("nt2", [P, 4, TT])
        second.close()

        consts_in = sem("consts_in")
        full, free = sems("bank_full", NBANK), sems("bank_free", NBANK)
        phase_done = sem("phase_done")
        dve_step = sem("dve_step")
        pool_step = sem("pool_step")
        x_loaded, x_stored = sems("x_loaded", 2), sems("x_stored", 2)
        xn_ready, xnt_ready, mix_ready = sem("xn_ready"), sem("xnt_ready"), sem("mix_ready")
        bias_added, x1_ready = sem("bias_added"), sem("x1_ready")
        sin_in, sin_out = sem("sin_in"), sem("sin_out")
        rot_ready, hi_ready, rem_ready, mid_ready, lo_ready = (
            sem("rot_ready"), sem("hi_ready"), sem("rem_ready"), sem("mid_ready"), sem("lo_ready"))
        parts_stored = sems("parts_stored", 4)
        relu_ready, kact_ready, gate_ready = sem("relu_ready"), sem("kact_ready"), sem("gate_ready")
        ones_set = sem("ones_set")
        stk_loaded, neg_loaded = sems("stk_loaded", NSTK), sems("neg_loaded", NSTK)
        st_full, st_free = sems("st_full", 2), sems("st_free", 2)
        mx_full, mx_free = sems("mx_full", 3), sems("mx_free", 3)
        pv_done = sems("pv_done", NP)
        po_free = sems("po_free", NSTK)
        v_ready = sem("v_ready")
        neg_ready = sem("neg_ready")
        o_stored = sems("o_stored", NSTK)
        w2_in = sem("w2_in")
        prep = sem("prep")
        x1_loaded, heads_loaded, out_stored = sems("x1_loaded", NC), sems("heads_loaded", 2), sems("out_stored", NC)
        at_ready, xn2_ready, xn2t_ready = sem("at_ready"), sem("xn2_ready"), sem("xn2t_ready")
        q2_ready, qk2_ready, v2_ready = sem("q2_ready"), sem("qk2_ready"), sem("v2_ready")
        lg_ready, lgs_ready, ex_ready, aw_ready = (
            sem("lg_ready"), sem("lgs_ready"), sem("ex_ready"), sem("aw_ready"))
        awn_ready = sem("awn_ready")
        state_ready, qs_ready, gate2_ready, o2_ready = (
            sem("state_ready"), sem("qs_ready"), sem("gate2_ready"), sem("o2_ready"))
        z2_ready, fb_ready, f2_ready, y_ready = (
            sem("z2_ready"), sem("fb_ready"), sem("f2_ready"), sem("y_ready"))

        def ring(order):
            assert len(order) % NBANK == 0
            return {name: (k % NBANK, k // NBANK) for k, name in enumerate(order)}, len(order) // NBANK

        order1 = [("t", 0, 0), ("t", 0, 1)]
        for c in range(NC):
            order1 += [("qk", c, j) for j in range(4)] + [("v", c, 0), ("v", c, 1)]
            order1 += [("fk", c, 0), ("fk", c, 1)]
            if c + 1 < NC:
                order1 += [("t", c + 1, 0), ("t", c + 1, 1)]
            order1 += [("r", c, 0), ("r", c, 1), ("fv", c, 0), ("fv", c, 1)]
        bank1, uses1 = ring(order1)

        def front3(c):
            return [("op", c, 0), ("op", c, 1)], [("t", c, 0), ("t", c, 1)]

        order3 = front3(0)[0] + front3(0)[1]
        for c in range(NC):
            order3 += [("q", c, j) for j in range(IT)] + [("k", c, j) for j in range(IT)]
            if c:
                order3 += [("wo", c - 1, 0), ("wo", c - 1, 1)]
            order3 += [("lg", c, 0)] + [("v", c, j) for j in range(IT)] + [("lt", c, 0)]
            if c + 1 < NC:
                order3 += front3(c + 1)[0]
            order3 += [("f", c, 0), ("f", c, 1)] + [("aw", c, j) for j in range(IT)]
            if c + 1 < NC:
                order3 += front3(c + 1)[1]
        order3 += [("wo", NC - 1, 0), ("wo", NC - 1, 1)]
        bank3, uses3 = ring(order3)
        used1 = uses1 * B
        before1 = [0] * NBANK
        before3 = [used1 + (bank < 2) for bank in range(NBANK)]

        class Banks:

            def __init__(self, eng, table, before, per_batch, batch):
                self.eng, self.table, self.before, self.batch = eng, table, before, per_batch * batch

            def count(self, item, more):
                bank, turn = self.table[item]
                return bank, self.batch + (self.before[bank] + turn + more)

            def claim(self, item):
                bank, count = self.count(item, 0)
                self.eng.wait_ge(free[bank], count)
                return psum[:, bank, :]

            def arrived(self, item):
                bank, count = self.count(item, 1)
                self.eng.wait_ge(full[bank], count)
                return psum[:, bank, :]

            def was_read(self, item):
                bank, count = self.count(item, 1)
                self.eng.wait_ge(free[bank], count)

            def full(self, item):
                return full[self.table[item][0]]

            def free(self, item):
                return free[self.table[item][0]]

        class Chain:
            def __init__(self, eng, step, base):
                self.eng, self.step, self.base, self.n = eng, step, base, 0

            def __call__(self, instruction):
                instruction.then_inc(self.step, 1)
                self.n += 1
                return self.n

            def wait(self, n=None):
                self.eng.wait_ge(self.step, self.base + (self.n if n is None else n))

        def end_phase(eng, n):
            eng.drain().then_inc(phase_done, 1)
            eng.wait_ge(phase_done, 5 * n)

        CHAIN1, CHAIN3 = 72, 144
        CHAIN2 = 3
        PCHAIN3 = 12

        AHEAD = 2

        def max_tile(g_off, s):
            return (g_off + 1, s + AHEAD) if s < KT - AHEAD else (g_off + 2, s + AHEAD - KT)

        LOOP = 20
        TAIL = [(LOOP, 0), (LOOP, 1), (LOOP, 2), (LOOP + 1, 0)]

        def exists(turn, g_off):
            return not isinstance(turn, int) or 3 * turn + g_off < NG

        block = top.enter_context(nc.Block())

        @block.sync
        def _(sp):
            for dst, src in ((w_qk, a["w_qk"]), (w_v, a["w_v"]), (wf_r, a["wf_r"]),
                             (wf_k, a["wf_k"]), (wf_v, a["wf_v"])):
                sp.dma_start(dst[:, :, :], src.rearrange("(t p) n -> p t n", p=P)).then_inc(consts_in, 16)
            sp.dma_start(mu[:, :, :], a["mu"]).then_inc(consts_in, 16)
            sp.dma_start(b_out[:, :], a["b_out"].partition_broadcast(P)).then_inc(consts_in, 16)
            sp.dma_start(ident[:, :], a["ident"]).then_inc(consts_in, 16)
            sp.dma_start(cos_t[:, :], a["cos"]).then_inc(consts_in, 16)
            sp.dma_start(sin_t[:, :], a["sin"]).then_inc(consts_in, 16)

            with sp.Fori(0, B) as b:
                def load(c):
                    p = c % 2
                    sp.wait_ge(x_stored[p], b * 32 + 16 * (c // 2))
                    src = x_rows[bass.ds(b * S + c * CH, CH), :]
                    sp.dma_start(x_in[p][:, :, :], src.rearrange("(t p) d -> p t d", p=P)).then_inc(x_loaded[p], 16)

                load(0)
                load(1)
                for c in range(NC):
                    for j in range(4):
                        dst, tile = ((scratch_q, j) if j < 2 else (scratch_k, j - 2))
                        sp.wait_ge(lo_ready, b * (4 * NC) + (4 * c + j + 1))
                        rows = dst[:, bass.ds(b * D + tile * P, P), c * CH:(c + 1) * CH]
                        sp.dma_start(rows.rearrange("a p t -> p a t"), parts[j][:, :, :]).then_inc(parts_stored[j], 16)
                    sp.wait_ge(x1_ready, b * NC + (c + 1))
                    dst = scratch_x[bass.ds(b * S + c * CH, CH), :]
                    sp.dma_start(dst.rearrange("(t p) d -> p t d", p=P), x_in[c % 2][:, :, :]).then_inc(x_stored[c % 2], 16)
                    if c + 2 < NC:
                        load(c + 2)
            for p in range(2):
                sp.wait_ge(x_stored[p], 16 * B * NC // 2)
            for j in range(4):
                sp.wait_ge(parts_stored[j], 16 * B * NC)
            end_phase(sp, 1)

            def load_stack(g, turn_before, j):
                for part0, n, row in ((0, 3, 0), (0, 2, 3 * HD), (0, 1, 5 * HD)):
                    for i in range(n):
                        src = scratch_q[part0 + i, bass.ds(g * HD, HD), :]
                        sp.dma_start(q_stk[j][row + i * HD:row + (i + 1) * HD, :], src).then_inc(stk_loaded[j], 16)
                for part, n, row in ((0, 3, 0), (1, 2, 3 * HD), (2, 1, 5 * HD)):
                    for i in range(n):
                        src = scratch_k[part, bass.ds(g * HD, HD), :]
                        sp.dma_start(k_stk[j][row + i * HD:row + (i + 1) * HD, :], src).then_inc(stk_loaded[j], 16)

            def load_neg(count, j):
                sp.wait_ge(neg_ready, count)
                for quad in range(4):
                    for half in range(2):
                        row = q_stk[j][ROWS + half:ROWS + half + 1, :].rearrange(
                            "p (t q i) -> p q t i", q=4, i=32)[:, quad]
                        base = 32 * quad + KT * half
                        sp.dma_start(row, neg_t[j][base:base + KT, :]).then_inc(neg_loaded[j], 16)

            sp.wait_ge(ones_set, 2)
            for g in range(NSTK):
                load_stack(g, 0, g)
            load_neg(1, 0)

            def head_io(turn, j):
                g = turn * 3 + j
                if exists(turn, j + 1):
                    load_neg(g + 2, (j + 1) % 3)
                if exists(turn, j + 3):
                    for n in range(2):
                        sp.wait_ge(st_full[n], g * KT + KT)
                    load_stack(g + 3, turn, j)
                sp.wait_ge(po_free[j], turn + 1)
                for c in range(4):
                    dst = scratch_o[bass.ds(g * 32, 32), c * 512:(c + 1) * 512]
                    sp.dma_start(dst, o_head[j][32 * c:32 * c + 32, :]).then_inc(o_stored[j], 16)

            with sp.Fori(0, LOOP) as turn:
                for j in range(3):
                    head_io(turn, j)
            for turn, j in TAIL:
                head_io(turn, j)
            for j in range(3):
                sp.wait_ge(o_stored[j], 64 * (LOOP + 1 + (j == 0)))
            end_phase(sp, 2)

            for n, name in (("q", "w2_q"), ("k", "w2_k"), ("v", "w2_v")):
                sp.dma_start(w2[n][:, :, :], a[name].rearrange("(t p) n -> p t n", p=P)).then_inc(w2_in, 16)
            for dst, name in ((w_out, "w_out"), (w_o2, "w_o2"), (wa["w"], "wa_w"), (wa["1"], "wa_1"), (wa["2"], "wa_2")):
                sp.dma_start(dst[:, :, :], a[name].rearrange("(t p) n -> p t n", p=P)).then_inc(w2_in, 16)
            sp.dma_start(col[:, :, :], a["col"]).then_inc(w2_in, 16)
            for i, name in enumerate(("bo", "f_bias", "ln_scale", "ln_bias")):
                sp.dma_start(row_bc[:, i, :], a[name].partition_broadcast(P)).then_inc(w2_in, 16)
            with sp.Fori(0, B) as b:
                def load_x(c):
                    sp.wait_ge(out_stored[c], b * 16)
                    src = scratch_x[bass.ds(b * S + c * CH, CH), :]
                    sp.dma_start(xc[c][:, :, :], src.rearrange("(t p) d -> p t d", p=P)).then_inc(x1_loaded[c], 16)

                def load_heads(c):
                    sp.wait_ge(xn2_ready, b * NC + max(c - 1, 0))
                    for ct in range(DT):
                        heads = scratch_o[bass.ds(b * (H * 32) + ct * (8 * 32), 8 * 32), c * CH:(c + 1) * CH]
                        heads = heads.rearrange("(h r) t -> h r t", r=32)
                        for dst, rows in ((a_raw, heads[:, 0:HD, :]), (a_sum, heads[:, HD:2 * HD, :])):
                            sp.dma_start(dst[c % 2][:, ct, :], rows).then_inc(heads_loaded[c % 2], 16)

                for c in range(NC):
                    load_x(c)
                    if c < 2:
                        load_heads(c)
                for c in range(NC):
                    if c + 2 < NC:
                        load_heads(c + 2)
                    sp.wait_ge(y_ready, b * NC + (c + 1))
                    dst = out_rows[bass.ds(b * S + c * CH, CH), :]
                    sp.dma_start(dst.rearrange("(t p) d -> p t d", p=P), xc[c][:, :, :]).then_inc(out_stored[c], 16)
            for c in range(NC):
                sp.wait_ge(out_stored[c], 16 * B)

        @block.tensor
        def _(pe):
            mm = nc.tensor.matmul

            def transposes(banks, item, source, pick):
                dst = banks.claim(item)
                for t in range(TT):
                    last = nc.tensor.transpose(dst[:, t * P:(t + 1) * P], pick(source, t), ident[:, :])
                last.then_inc(banks.full(item), 1)

            def by_channel(banks, item, weights, cols, moving, n_k, offset=0):
                dst = banks.claim(item)
                for kt in range(n_k):
                    last = mm(dst, weights[:, kt, cols], moving[:, kt, offset:offset + CH],
                              start=(kt == 0), stop=(kt == n_k - 1))
                last.then_inc(banks.full(item), 1)

            def by_token(banks, item, pair, stationary, weights, n_k, offset=0):
                dst = banks.claim(item)
                for i in range(2):
                    t0 = offset + (2 * pair + i) * P
                    for kt in range(n_k):
                        last = mm(dst[:, i * D:(i + 1) * D], stationary[:, kt, t0:t0 + P],
                                  weights[:, kt, :], start=(kt == 0), stop=(kt == n_k - 1))
                last.then_inc(banks.full(item), 1)

            pe.wait_ge(consts_in, 10 * 16)
            with pe.Fori(0, B) as b:
                banks = Banks(pe, bank1, before1, uses1, b)

                def xn_transposes(c):
                    pe.wait_ge(xn_ready, b * NC + (c + 1))
                    for ct in range(DT):
                        transposes(banks, ("t", c, ct), xn[c % 2],
                                   lambda src, t: src[:, t, ct * P:(ct + 1) * P])

                xn_transposes(0)
                for c in range(NC):
                    p = c % 2
                    pe.wait_ge(xnt_ready, b * NC + (c + 1))
                    for j in range(4):
                        by_channel(banks, ("qk", c, j), w_qk, slice(j * P, (j + 1) * P), xn_t[p], DT, 1)
                    for pair in range(2):
                        by_token(banks, ("v", c, pair), pair, xn_t[p], w_v, DT, 1)
                    pe.wait_ge(mix_ready, b * NC + (c + 1))
                    for j in range(DT):
                        by_channel(banks, ("fk", c, j), wf_k, slice(j * P, (j + 1) * P), x_mix[p][:, 1], DT)
                    if c + 1 < NC:
                        xn_transposes(c + 1)
                    for pair in range(2):
                        by_token(banks, ("r", c, pair), pair, x_mix[p][:, 0], wf_r, DT)
                    pe.wait_ge(kact_ready, b * NC + (c + 1))
                    for pair in range(2):
                        by_token(banks, ("fv", c, pair), pair, k_act, wf_v, DT)
            end_phase(pe, 1)

            for bank in range(NBANK):
                pe.wait_ge(free[bank], used1)

            def max_scores(turn, g_off, tile, c):
                j, m = g_off % 3, 4 * KT * g_off + 4 * tile + c
                if tile == 0 and c == 0:
                    pe.wait_ge(stk_loaded[j], (turn + g_off // 3) * (12 * 16) + 12 * 16)
                pe.wait_ge(mx_free[m % 3], turn * (4 * KT) + m // 3)
                mm(psum[:, 4 + m % 3, :], q_stk[j][0:ROWS, tile * P:(tile + 1) * P],
                   k_stk[j][0:ROWS, c * 512:(c + 1) * 512], start=True, stop=True).then_inc(mx_full[m % 3], 1)

            def scores(turn, j, kt, half):
                pe.wait_ge(st_free[half], (turn * 3 + j) * KT + kt)
                for c in (2 * half, 2 * half + 1):
                    last = mm(psum[:, c, :], k_stk[j][0:ROWS + 2, kt * P:(kt + 1) * P],
                              q_stk[j][0:ROWS + 2, c * 512:(c + 1) * 512], start=True, stop=True)
                last.then_inc(st_full[half], 1)

            def weigh(turn, j, kt):
                for half in range(2):
                    pe.wait_ge(st_free[half], (turn * 3 + j) * KT + kt + 1)
                if kt == 0:
                    pe.wait_ge(v_ready, turn * 3 + j + 1)
                    pe.wait_ge(po_free[(j - 1) % 3], turn + (j > 0))
                for c in range(4):
                    last = mm(psum[32 * c:32 * c + 32, 7, :], v_head[j][:, kt, :],
                              probs[kt % NP][:, c * 512:(c + 1) * 512], start=(kt == 0), stop=(kt == KT - 1))
                last.then_inc(pv_done[kt % NP], 1)

            pe.wait_ge(ones_set, 2)
            for tile in range(KT + AHEAD):
                for c in range(4):
                    max_scores(0, tile // KT, tile % KT, c)

            def head(turn, j):
                pe.wait_ge(neg_loaded[j], turn * (8 * 16) + 8 * 16)
                for kt in range(KT):
                    g_off, tile = max_tile(j, kt)
                    for half in range(2):
                        scores(turn, j, kt, half)
                        if exists(turn, g_off):
                            for c in (2 * half, 2 * half + 1):
                                max_scores(turn, g_off, tile, c)
                    if kt:
                        weigh(turn, j, kt - 1)
                weigh(turn, j, KT - 1)

            with pe.Fori(0, LOOP) as turn:
                for j in range(3):
                    head(turn, j)
            for turn, j in TAIL:
                head(turn, j)
            end_phase(pe, 2)

            pe.wait_ge(w2_in, 13 * 16)
            for name, lhs_t, rhs, bank in (("12", wa["1"], wa["2"], 0), ("f", wa["w"], w_12, 1)):
                if name == "f":
                    pe.wait_ge(free[0], used1 + 1)
                for j in range(DT):
                    for kt in range(DT):
                        last = mm(psum[:, bank, j * D:(j + 1) * D], lhs_t[:, kt, j * P:(j + 1) * P],
                                  rhs[:, kt, :], start=(kt == 0), stop=(kt == DT - 1))
                last.then_inc(full[bank], 1)
            pe.wait_ge(free[1], used1 + 1)
            pe.wait_ge(prep, 1)
            with pe.Fori(0, B) as b:
                banks = Banks(pe, bank3, before3, uses3, b)
                def project_out(c):
                    pe.wait_ge(at_ready, b * NC + (c + 1))
                    for pair in range(2):
                        by_token(banks, ("op", c, pair), pair, a_raw[c % 2], w_out, DT)

                def xn_transposes2(c):
                    pe.wait_ge(xn2_ready, b * NC + (c + 1))
                    for ct in range(DT):
                        transposes(banks, ("t", c, ct), xn2, lambda src, t: src[:, t, ct * P:(ct + 1) * P])

                def output2(c):
                    pe.wait_ge(o2_ready, b * NC + (c + 1))
                    for pair in range(2):
                        by_token(banks, ("wo", c, pair), pair, o2, w_o2, IT)

                project_out(0)
                xn_transposes2(0)
                for c in range(NC):
                    p = c % 2
                    pe.wait_ge(xn2t_ready, b * NC + (c + 1))
                    for j in range(IT):
                        by_channel(banks, ("q", c, j), w2["q"], slice(j * P, (j + 1) * P), xn2_t[p], DT)
                    for j in range(IT):
                        by_channel(banks, ("k", c, j), w2["k"], slice(j * P, (j + 1) * P), xn2_t[p], DT)
                    if c:
                        output2(c - 1)
                    pe.wait_ge(qk2_ready, b * NC + (c + 1))
                    dst = banks.claim(("lg", c, 0))
                    for j in range(IT):
                        last = mm(dst[32 * j:32 * j + 32, :], head_sel[:, :], qk2[:, j, :], start=True, stop=True)
                    last.then_inc(banks.full(("lg", c, 0)), 1)
                    for j in range(IT):
                        by_channel(banks, ("v", c, j), w2["v"], slice(j * P, (j + 1) * P), xn2_t[p], DT)
                    pe.wait_ge(lg_ready, b * NC + (c + 1))
                    transposes(banks, ("lt", c, 0), lg, lambda src, t: src[:, t * P:(t + 1) * P])
                    if c + 1 < NC:
                        project_out(c + 1)
                    for pair in range(2):
                        by_token(banks, ("f", c, pair), pair, xn2_t[p], w_ffn, DT)
                    pe.wait_ge(aw_ready, b * NC + (c + 1))
                    for j in range(IT):
                        transposes(banks, ("aw", c, j), aw_wide,
                                   lambda src, t: src[:, t, 2 * HD2 * j:2 * HD2 * (j + 1)])
                    if c + 1 < NC:
                        xn_transposes2(c + 1)
                output2(NC - 1)

        @block.scalar
        def _(act):
            def copy(dst, src):
                return nc.scalar.activation(dst, src, ACT.Copy)

            with act.Fori(0, B) as b:
                banks = Banks(act, bank1, before1, uses1, b)

                def evacuate_t(c):
                    p = c % 2
                    for ct in range(DT):
                        item = ("t", c, ct)
                        copy(xn_t[p][:, ct, 1:CH + 1], banks.arrived(item)).then_inc(banks.free(item), 1)
                    if c == 0:
                        nc.scalar.activation(xn_t[p][:, :, 0:1], ident[:, 0:DT].unsqueeze(2), ACT.Copy, scale=0.0)
                    else:
                        act.wait_ge(xnt_ready, b * NC + c)
                        copy(xn_t[p][:, :, 0:1], xn_t[1 - p][:, :, CH:CH + 1])
                    act.drain().then_inc(xnt_ready, 1)

                def split_hi(c, j):
                    act.wait_ge(rot_ready, b * (4 * NC) + (4 * c + j + 1))
                    act.wait_ge(parts_stored[j], b * (16 * NC) + 16 * c)
                    copy(parts[j][:, 0, :], r_cos[j][:, :]).then_inc(hi_ready, 1)

                def split_mid(c, j):
                    act.wait_ge(rem_ready, b * (4 * NC) + (4 * c + j + 1))
                    copy(parts[j][:, 1, :], r_cos[j][:, :]).then_inc(mid_ready, 1)

                act.wait_ge(consts_in, 10 * 16)
                evacuate_t(0)
                for c in range(NC):
                    for j in range(4):
                        split_hi(c, j)
                        if j:
                            split_mid(c, j - 1)
                    split_mid(c, 3)
                    for pair in range(2):
                        item = ("v", c, pair)
                        src = banks.arrived(item).rearrange("p (t h d) -> p t h d", t=2, h=H)
                        for i in range(2):
                            dst = v_all[:, bass.ds(b * H, H), c * TT + 2 * pair + i, :]
                            last = copy(dst, src[:, i])
                        last.then_inc(banks.free(item), 1)
                    for j in range(DT):
                        item = ("fk", c, j)
                        nc.scalar.activation(k_act[:, j, :], banks.arrived(item), ACT.Relu).then_inc(banks.free(item), 1)
                    act.drain().then_inc(relu_ready, 1)
                    if c + 1 < NC:
                        evacuate_t(c + 1)
                    for pair in range(2):
                        item = ("r", c, pair)
                        src = banks.arrived(item)
                        nc.scalar.activation(r_gate[pair][:, :], src, ACT.Tanh, scale=0.5).then_inc(banks.free(item), 1)
                    act.drain().then_inc(gate_ready, 1)
            end_phase(act, 1)

            def exponentials(turn, j, kt, half):
                g = turn * 3 + j
                if half == 0:
                    act.wait_ge(pv_done[kt % NP], g * (KT // NP) + kt // NP)
                act.wait_ge(st_full[half], g * KT + (kt + 1))
                nc.scalar.activation(probs[kt % NP][:, half * 1024:(half + 1) * 1024].rearrange("p (c q) -> p c q", c=2),
                                     psum[:, 2 * half:2 * half + 2, :], ACT.Exp, scale=HD ** -0.5).then_inc(st_free[half], 1)

            def copy_output(turn, j):
                g = turn * 3 + j
                act.wait_ge(o_stored[j], turn * 64)
                act.wait_ge(pv_done[(KT - 1) % NP], g * (KT // NP) + KT // NP)
                copy(o_head[j][:, :], psum[:, 7, :]).then_inc(po_free[j], 1)

            def head(turn, j):
                for kt in range(KT):
                    for half in range(2):
                        exponentials(turn, j, kt, half)
                copy_output(turn, j)

            with act.Fori(0, LOOP) as turn:
                for j in range(3):
                    head(turn, j)
            for turn, j in TAIL:
                head(turn, j)
            end_phase(act, 2)

            for bank, dst in ((0, w_12), (1, w_ffn)):
                act.wait_ge(full[bank], used1 + 1)
                copy(dst[:, :, :], psum[:, bank, :].rearrange("p (j n) -> p j n", j=DT)).then_inc(free[bank], 1)
            act.wait_ge(w2_in, 13 * 16)
            nc.scalar.activation(decay[:, :], col[:, 3, :], ACT.Tanh, scale=0.5).then_inc(gate2_ready, 1)
            act.wait_ge(prep, 1)
            with act.Fori(0, B) as b:
                banks = Banks(act, bank3, before3, uses3, b)

                def evacuate_t2(c):
                    for ct in range(DT):
                        item = ("t", c, ct)
                        copy(xn2_t[c % 2][:, ct, :], banks.arrived(item)).then_inc(banks.free(item), 1)
                    act.drain().then_inc(xn2t_ready, 1)

                evacuate_t2(0)
                for c in range(NC):
                    act.wait_ge(o2_ready, b * NC + c)
                    for j in range(IT):
                        item = ("q", c, j)
                        nc.scalar.activation(q2[:, j, :], banks.arrived(item), ACT.Identity,
                                             bias=col[:, 0, j:j + 1]).then_inc(banks.free(item), 1)
                    act.drain().then_inc(q2_ready, 1)
                    for j in range(IT):
                        last = nc.scalar.activation(gate2[:, j, :], q2[:, j, :], ACT.Tanh, scale=half_aug[:, j:j + 1])
                    last.then_inc(gate2_ready, 1)
                    item = ("lg", c, 0)
                    nc.scalar.activation(lg[:, :], banks.arrived(item), ACT.Copy, scale=HD2 ** -0.5).then_inc(banks.free(item), 1)
                    act.drain().then_inc(lg_ready, 1)
                    for j in range(IT):
                        item = ("v", c, j)
                        nc.scalar.activation(v2[:, j, :], banks.arrived(item), ACT.Identity,
                                             bias=v_bias[:, j:j + 1], scale=v_scale[:, j:j + 1]).then_inc(banks.free(item), 1)
                    act.drain().then_inc(v2_ready, 1)
                    act.wait_ge(lgs_ready, b * NC + (c + 1))
                    nc.scalar.activation(aw[:, :, :], aw[:, :, :], ACT.Exp).then_inc(ex_ready, 1)
                    act.wait_ge(awn_ready, b * NC + (c + 1))
                    nc.scalar.activation(aw_wide[:, :, :].rearrange("p t (h d) -> p t h d", h=H2),
                                         aw[:, :, :].unsqueeze(3).to_broadcast([P, TT, H2, HD2]),
                                         ACT.Copy).then_inc(aw_ready, 1)
                    if c + 1 < NC:
                        evacuate_t2(c + 1)
                    act.wait_ge(fb_ready, b * NC + (c + 1))
                    nc.scalar.activation(f2[:, :, :], f2[:, :, :], ACT.Tanh).then_inc(f2_ready, 1)

        @block.vector
        def _(dve):
            v = nc.vector

            def rsqrt(chain, var, nt, eps):
                val, y, tmp, half = nt[:, 0], nt[:, 1], nt[:, 2], nt[:, 3]
                chain(v.tensor_scalar(val, var, eps, None, ALU.add))
                chain.wait()
                v.tensor_scalar(half, val, -0.5, None, ALU.mult)
                chain(v.tensor_scalar(y.bitcast(I32), val.bitcast(I32), 1, None, ALU.logical_shift_right))
                chain.wait()
                chain(v.tensor_scalar(y.bitcast(I32), y.bitcast(I32), -1.0, float(RSQRT_SEED), ALU.mult, ALU.add))
                chain.wait()
                for _ in range(3):
                    chain(v.tensor_tensor(tmp, y, y, ALU.mult))
                    chain.wait()
                    chain(v.tensor_tensor(tmp, tmp, half, ALU.mult))
                    chain.wait()
                    chain(v.scalar_tensor_tensor(y, tmp, 1.5, y, ALU.add, ALU.mult))
                    chain.wait()
                return y

            def normalise(chain, src, dst, stats, mv, nt, eps):
                for t in range(TT):
                    v.bn_stats(stats[:, t, :], src[:, t, :])
                dve.drain()
                for t in range(TT):
                    chain(v.bn_aggr(mv[:, t, :], stats[:, t, :]))
                chain.wait()
                rstd = rsqrt(chain, mv[:, :, 1], nt, eps)
                for t in range(TT):
                    last = v.tensor_scalar(dst[:, t, :], src[:, t, :], mv[:, t, 0:1], rstd[:, t:t + 1],
                                           ALU.subtract, ALU.mult)
                return last

            swap = [(p ^ (HD // 2)) for p in range(32)]

            dve.wait_ge(consts_in, 10 * 16)
            with dve.Fori(0, B) as b:
                banks = Banks(dve, bank1, before1, uses1, b)
                chain = Chain(dve, dve_step, b * CHAIN1)

                def norm(c):
                    p = c % 2
                    dve.wait_ge(x_loaded[p], b * 32 + 16 * (c // 2 + 1))
                    if c >= 2:
                        dve.wait_ge(xnt_ready, b * NC + (c - 1))
                    normalise(chain, x_in[p], xn[p], stats1, mv1, nt1, EPS1).then_inc(xn_ready, 1)

                def rotate(c, j):
                    item = ("qk", c, j)
                    src = banks.arrived(item)
                    v.tensor_tensor(r_cos[j][:, :], src, cos_t[:, c * CH:(c + 1) * CH], ALU.mult)
                    v.stream_shuffle(r_sin[j][:, :], src, swap).then_inc(banks.free(item), 1)
                    dve.drain().then_inc(sin_in, 1)

                def add(c, j):
                    dve.wait_ge(sin_out, b * (4 * NC) + (4 * c + j + 1))
                    v.tensor_tensor(r_cos[j][:, :], r_cos[j][:, :], r_sin[j][:, :], ALU.add).then_inc(rot_ready, 1)

                def remainder(c, j):
                    dve.wait_ge(hi_ready, b * (4 * NC) + (4 * c + j + 1))
                    v.tensor_tensor(r_cos[j][:, :], r_cos[j][:, :], parts[j][:, 0, :], ALU.subtract).then_inc(rem_ready, 1)

                def low(c, j):
                    dve.wait_ge(mid_ready, b * (4 * NC) + (4 * c + j + 1))
                    v.tensor_tensor(parts[j][:, 2, :], r_cos[j][:, :], parts[j][:, 1, :], ALU.subtract).then_inc(lo_ready, 1)

                norm(0)
                for c in range(NC):
                    p = c % 2
                    for i in range(4 + 3):
                        if i < 4:
                            rotate(c, i)
                        if 0 <= i - 1 < 4:
                            add(c, i - 1)
                        if 0 <= i - 2 < 4:
                            remainder(c, i - 2)
                        if 0 <= i - 3 < 4:
                            low(c, i - 3)
                    if c + 1 < NC:
                        norm(c + 1)
                    dve.wait_ge(gate_ready, b * NC + (c + 1))
                    dve.wait_ge(bias_added, b * NC + (c + 1))
                    for pair in range(2):
                        item = ("fv", c, pair)
                        dst = x_in[p][:, 2 * pair:2 * pair + 2, :].rearrange("p t d -> p (t d)")
                        chain(v.scalar_tensor_tensor(r_gate[pair][:, :], r_gate[pair][:, :], 1.0, banks.arrived(item),
                                                     ALU.add, ALU.mult))
                        chain.wait()
                        last = v.scalar_tensor_tensor(dst, r_gate[pair][:, :], 0.5, dst, ALU.mult, ALU.add)
                        last.then_inc(banks.free(item), 1)
                    dve.drain().then_inc(x1_ready, 1)
                assert chain.n == CHAIN1, chain.n
            chained1 = B * CHAIN1
            end_phase(dve, 1)

            def maxima(turn, g_off, tile, c):
                m = 4 * KT * g_off + 4 * tile + c
                dve.wait_ge(mx_full[m % 3], turn * (4 * KT) + (m // 3 + 1))
                v.tensor_reduce(max_part[g_off % 3][:, tile, c:c + 1], psum[:, 4 + m % 3, :], AX.X, ALU.max)\
                    .then_inc(mx_free[m % 3], 1)

            def shift_rows(turn, g_off):
                chain = Chain(dve, dve_step, turn * (3 * CHAIN2) + (chained1 + g_off * CHAIN2))
                j = g_off % 3
                for r in range(3):
                    top = 4 * KT * (g_off + 1) - 1
                    m = top - (top - r) % 3
                    dve.wait_ge(mx_free[r], turn * (4 * KT) + (m // 3 + 1))
                chain(v.tensor_reduce(neg_max[:, :], max_part[j][:, :, :], AX.X, ALU.max, negate=True))
                chain.wait()
                chain(v.tensor_copy(neg_hl[:, 0, :], neg_max[:, :]))
                chain.wait()
                chain(v.tensor_tensor(neg_hl[:, 1, :], neg_max[:, :], neg_hl[:, 0, :], ALU.subtract))
                chain.wait()
                v.transpose(neg_t[j][:, :], neg_hl[:, :, :].rearrange("p a t -> p (a t)")).then_inc(neg_ready, 1)
                assert chain.n == CHAIN2

            for tile in range(KT + AHEAD):
                for c in range(4):
                    maxima(0, tile // KT, tile % KT, c)
                if tile == KT - 1:
                    shift_rows(0, 0)

            def head(turn, j):
                for s in range(KT):
                    g_off, tile = max_tile(j, s)
                    if exists(turn, g_off):
                        for c in range(4):
                            maxima(turn, g_off, tile, c)
                        if tile == KT - 1:
                            shift_rows(turn, g_off)

            with dve.Fori(0, LOOP) as turn:
                for j in range(3):
                    head(turn, j)
            for turn, j in TAIL:
                head(turn, j)
            chained2 = chained1 + NG * CHAIN2
            end_phase(dve, 2)

            dve.wait_ge(gate2_ready, 1)
            dve.wait_ge(w2_in, 13 * 16)
            setup = Chain(dve, dve_step, chained2)
            v.memset(head_sel[:, :], 0.0)
            setup(v.tensor_scalar(v_scale[:, :], decay[:, :], -1.0, 1.0, ALU.mult, ALU.add))
            setup(v.tensor_scalar(decay[:, :], decay[:, :], 0.5, 0.5, ALU.mult, ALU.add))
            setup.wait()
            v.memset(head_sel[0:HD2, 0:1], 1.0)
            v.memset(head_sel[HD2:P, 1:2], 1.0)
            v.tensor_scalar(half_aug[:, :], col[:, 4, :], 0.5, None, ALU.mult)
            v.tensor_tensor(v_bias[:, :], v_scale[:, :], col[:, 2, :], ALU.mult)
            dve.drain().then_inc(prep, 1)
            chained3 = chained2 + setup.n
            with dve.Fori(0, B) as b:
                banks = Banks(dve, bank3, before3, uses3, b)
                chain = Chain(dve, dve_step, b * CHAIN3 + chained3)

                def attention_normal(c):
                    p = c % 2
                    dve.wait_ge(heads_loaded[p], b * (2 * 64) + 64 * (c // 2 + 1))
                    chain(v.reciprocal(a_sum[p][:, :, :], a_sum[p][:, :, :]))
                    chain.wait()
                    v.tensor_tensor(a_raw[p][:, :, :], a_raw[p][:, :, :], a_sum[p][:, :, :], ALU.mult).then_inc(at_ready, 1)

                def residual_norm(c):
                    dve.wait_ge(x1_loaded[c], b * 16 + 16)
                    for pair in range(2):
                        item = ("op", c, pair)
                        dst = xc[c][:, 2 * pair:2 * pair + 2, :].rearrange("p t d -> p (t d)")
                        v.tensor_tensor(dst, banks.arrived(item), dst, ALU.add).then_inc(banks.free(item), 1)
                    banks.was_read(("op", c, 0))
                    banks.was_read(("op", c, 1))
                    if c:
                        dve.wait_ge(xn2t_ready, b * NC + c)
                    normalise(chain, xc[c], xn2, stats2, mv2, nt2, EPS1).then_inc(xn2_ready, 1)

                def output_norm(c):
                    dve.wait_ge(y_ready, b * NC + c)
                    for pair in range(2):
                        item = ("wo", c, pair)
                        src = banks.arrived(item).rearrange("p (t d) -> p t d", t=2)
                        v.scalar_tensor_tensor(z2[:, 2 * pair:2 * pair + 2, :], src, 0.5,
                                               row_bc[:, 0:1, :].to_broadcast([P, 2, D]),
                                               ALU.mult, ALU.add).then_inc(banks.free(item), 1)
                    banks.was_read(("wo", c, 0))
                    banks.was_read(("wo", c, 1))
                    normalise(chain, z2, z2, stats2, mv2, nt2, EPS2).then_inc(z2_ready, 1)

                attention_normal(0)
                residual_norm(0)
                for c in range(NC):
                    p = c % 2
                    dve.wait_ge(q2_ready, b * NC + (c + 1))
                    for j in range(IT):
                        item = ("k", c, j)
                        v.scalar_tensor_tensor(qk2[:, j, :], banks.arrived(item), col[:, 1, j:j + 1], q2[:, j, :],
                                               ALU.add, ALU.mult).then_inc(banks.free(item), 1)
                    dve.drain().then_inc(qk2_ready, 1)
                    if c + 1 < NC:
                        attention_normal(c + 1)
                    if c:
                        output_norm(c - 1)
                    item = ("lt", c, 0)
                    src = banks.arrived(item).rearrange("p (t j e) -> p t j e", t=TT, j=IT)[:, :, :, 0:2]
                    chain(v.tensor_reduce(aw_small[:, 0, :], src, AX.XY, ALU.max))
                    chain.wait()
                    for t in range(TT):
                        last = v.tensor_scalar(aw[:, t, :].rearrange("p (j e) -> p j e", e=2), src[:, t],
                                               aw_small[:, 0, t:t + 1], None, ALU.subtract)
                    last.then_inc(banks.free(item), 1)
                    dve.drain().then_inc(lgs_ready, 1)
                    dve.wait_ge(ex_ready, b * NC + (c + 1))
                    chain(v.tensor_reduce(aw_small[:, 1, :], aw[:, :, :], AX.X, ALU.add))
                    chain.wait()
                    chain(v.reciprocal(aw_small[:, 2, :], aw_small[:, 1, :]))
                    chain.wait()
                    v.tensor_tensor(aw[:, :, :], aw[:, :, :],
                                    aw_small[:, 2, :].unsqueeze(2).to_broadcast([P, TT, H2]), ALU.mult).then_inc(awn_ready, 1)
                    if c + 1 < NC:
                        residual_norm(c + 1)
                    dve.wait_ge(y_ready, b * NC + c)
                    for pair in range(2):
                        item = ("f", c, pair)
                        src = banks.arrived(item).rearrange("p (t d) -> p t d", t=2)
                        v.tensor_tensor(f2[:, 2 * pair:2 * pair + 2, :], src,
                                        row_bc[:, 1:2, :].to_broadcast([P, 2, D]), ALU.add).then_inc(banks.free(item), 1)
                    dve.drain().then_inc(fb_ready, 1)
                    dve.wait_ge(v2_ready, b * NC + (c + 1))
                    for j in range(IT):
                        item = ("aw", c, j)
                        v.tensor_tensor(v2[:, j, :], v2[:, j, :], banks.arrived(item), ALU.mult)\
                            .then_inc(banks.free(item), 1)
                        banks.was_read(item)
                        start = 0.0 if c == 0 else state[1 - p][:, j, CH - 1:CH]
                        v.tensor_tensor_scan(state[p][:, j, :], decay[:, j:j + 1].to_broadcast([P, CH]), v2[:, j, :],
                                             start, ALU.mult, ALU.add).then_inc(state_ready, 1)
                    dve.wait_ge(gate2_ready, b * NC + (c + 2))
                    dve.wait_ge(qs_ready, b * NC + (c + 1))
                    v.scalar_tensor_tensor(o2[:, :, :].rearrange("p j t -> p (j t)"),
                                           gate2[:, :, :].rearrange("p j t -> p (j t)"), 1.0,
                                           o2[:, :, :].rearrange("p j t -> p (j t)"),
                                           ALU.add, ALU.add).then_inc(o2_ready, 1)
                output_norm(NC - 1)
                assert chain.n == CHAIN3, chain.n

        @block.gpsimd
        def _(pool):
            g_ = nc.gpsimd
            pool.wait_ge(consts_in, 10 * 16)
            with pool.Fori(0, B) as b:
                def mix(c):
                    p = c % 2
                    pool.wait_ge(xnt_ready, b * NC + (c + 1))
                    now, before = xn_t[p][:, :, 1:CH + 1], xn_t[p][:, :, 0:CH]
                    g_.tensor_tensor(x_dif[:, :, :], now, before, ALU.subtract)
                    pool.drain()
                    for which in (1, 0):
                        for ct in range(DT):
                            g_.tensor_scalar(x_mix[p][:, which, ct, :], x_dif[:, ct, :], mu[:, which, ct:ct + 1], None, ALU.mult)
                    pool.drain()
                    for which in (1, 0):
                        last = g_.tensor_tensor(x_mix[p][:, which], x_mix[p][:, which], before, ALU.add)
                    last.then_inc(mix_ready, 1)

                mix(0)
                for c in range(NC):
                    for j in range(4):
                        pool.wait_ge(sin_in, b * (4 * NC) + (4 * c + j + 1))
                        g_.tensor_tensor(r_sin[j][:, :], r_sin[j][:, :], sin_t[:, c * CH:(c + 1) * CH], ALU.mult)\
                            .then_inc(sin_out, 1)
                    pool.wait_ge(relu_ready, b * NC + (c + 1))
                    g_.tensor_tensor(k_act[:, :, :], k_act[:, :, :], k_act[:, :, :], ALU.mult).then_inc(kact_ready, 1)
                    if c + 1 < NC:
                        mix(c + 1)
                    pool.wait_ge(xn_ready, b * NC + (c + 1))
                    g_.tensor_tensor(x_in[c % 2][:, :, :], x_in[c % 2][:, :, :],
                                     b_out[:, :].unsqueeze(1).to_broadcast([P, TT, D]), ALU.add).then_inc(bias_added, 1)
            end_phase(pool, 1)

            for j in range(NSTK):
                g_.memset(k_stk[j][ROWS:ROWS + 2, :], 1.0)
            pool.drain().then_inc(ones_set, 1)
            for j in range(NSTK):
                g_.memset(v_head[j][:, :, HD:], 1.0)
            pool.drain().then_inc(ones_set, 1)

            def head(turn, j):
                pool.wait_ge(po_free[j], turn)
                g_.tensor_copy(v_head[j][:, :, 0:HD], v_all[:, bass.ds(turn * 3 + j, 1), :, :].squeeze(1)
                               if not isinstance(turn, int) else v_all[:, turn * 3 + j, :, :]).then_inc(v_ready, 1)

            with pool.Fori(0, LOOP) as turn:
                for j in range(3):
                    head(turn, j)
            for turn, j in TAIL:
                head(turn, j)
            end_phase(pool, 2)

            with pool.Fori(0, B) as b:
                chain = Chain(pool, pool_step, b * PCHAIN3)

                def finish(c):
                    xp = xc[c]
                    pool.wait_ge(f2_ready, b * NC + (c + 1))
                    chain(g_.tensor_tensor(xp[:, :, :], xp[:, :, :], f2[:, :, :], ALU.add))
                    pool.wait_ge(z2_ready, b * NC + (c + 1))
                    chain(g_.tensor_tensor(z2[:, :, :], z2[:, :, :], row_bc[:, 2:3, :].to_broadcast([P, TT, D]), ALU.mult))
                    chain.wait()
                    chain(g_.tensor_tensor(z2[:, :, :], z2[:, :, :], row_bc[:, 3:4, :].to_broadcast([P, TT, D]), ALU.add))
                    chain.wait()
                    g_.tensor_tensor(xp[:, :, :], xp[:, :, :], z2[:, :, :], ALU.add).then_inc(y_ready, 1)

                for c in range(NC):
                    if c:
                        finish(c - 1)
                    for j in range(IT):
                        pool.wait_ge(state_ready, b * (IT * NC) + (IT * c + j + 1))
                        last = g_.tensor_tensor(o2[:, j, :], q2[:, j, :], state[c % 2][:, j, :], ALU.mult)
                    last.then_inc(qs_ready, 1)
                finish(NC - 1)
                assert chain.n == PCHAIN3, chain.n


def kernel(**inputs):
    import concourse.bacc as bacc
    from concourse.bass_utils import run_bass_kernel_spmd

    i = {k: np.asarray(x) for k, x in inputs.items()}
    order = np.concatenate([h * HD + np.concatenate([np.arange(0, HD, 2), np.arange(1, HD, 2)]) for h in range(H)])
    w = i["L0_attn_w_qkv"]

    def columns(*names):
        return np.stack([i[n].reshape(-1, P).T for n in names], axis=1)

    inv_freq = (1.0 / np.float32(10000.0) ** (np.arange(0, HD, 2, dtype=np.float32) / np.float32(HD))).astype(np.float32)
    angle = np.outer(np.arange(S, dtype=np.float32), inv_freq).astype(np.float32)
    row = np.arange(P) % HD
    cos = np.cos(angle).T[row % (HD // 2)]
    sin = np.sin(angle).T[row % (HD // 2)] * np.where(row < HD // 2, -1, 1)[:, None]
    arrays = {
        "x": i["L0_attn_x"],
        "w_qk": np.concatenate([w[0:D][order], w[D:2 * D][order]]).T,
        "w_v": w[2 * D:].T, "w_out": i["L0_attn_w_out"].T, "b_out": i["L0_attn_b_out"],
        "wf_r": i["L0_ffn_W_r"].T, "wf_k": i["L0_ffn_W_k"].T, "wf_v": i["L0_ffn_W_v"].T,
        "mu": columns("L0_ffn_mu_r", "L0_ffn_mu_k"),
        "cos": cos.astype(np.float32), "sin": sin.astype(np.float32), "ident": np.eye(P, dtype=np.float32),
        "w2_q": i["L1_attn_Wq"], "w2_k": i["L1_attn_Wk"], "w2_v": i["L1_attn_Wv"], "w_o2": i["L1_attn_Wo"],
        "col": columns("L1_attn_bq", "L1_attn_bk", "L1_attn_bv", "L1_attn_alpha", "L1_attn_aug_param"),
        "bo": i["L1_attn_bo"],
        "ln_scale": i["L1_attn_ln_scale"], "ln_bias": i["L1_attn_ln_bias"],
        "wa_w": i["L1_ffn_weight"].T, "wa_1": i["L1_ffn_aux_weight1"].T, "wa_2": i["L1_ffn_aux_weight2"],
        "f_bias": i["L1_ffn_bias"],
    }
    arrays = {k: np.ascontiguousarray(x) for k, x in arrays.items()}
    nc = bacc.Bacc("TRN2", target_bir_lowering=False, num_devices=1)
    aps = {k: nc.dram_tensor(f"in_{k}", x.shape, mybir.dt.from_np(x.dtype), kind="ExternalInput").ap()
           for k, x in arrays.items()}
    out = nc.dram_tensor("out_x", (B, S, D), F32, kind="ExternalOutput").ap()
    build(nc, aps, out)
    r = run_bass_kernel_spmd(nc, [{f"in_{k}": x for k, x in arrays.items()}], core_ids=[0])
    return r.results[0]["out_x"]
```

```python
import numpy as np
from contextlib import ExitStack

import concourse.bass as bass
from concourse import mybir

F32 = mybir.dt.float32
BF16 = mybir.dt.bfloat16
I32 = mybir.dt.int32
ALU = mybir.AluOpType
ACT = mybir.ActivationFunctionType
AX = mybir.AxisListType

P = 128
B, S, D = 4, 2048, 256
H, HD = 16, 16
NG = B * H
CH = 512
NC = S // CH
TT = CH // P
KT = S // P
DT = D // P
INNER = 512
H2, HD2 = 8, 64
IT = INNER // P
EPS1, EPS2 = 1e-5, 1e-6
NPARTS = 3
ROWS = 6 * HD
NBANK = 8
RSQRT_SEED = 0x5F3759DF
OPEN, OPEN_DMA = 1, 16


def build(nc, a, out):
    scratch_q = nc.dram_tensor("scratch_q", [NPARTS, B * D, S], BF16, kind="Internal").ap()
    scratch_k = nc.dram_tensor("scratch_k", [NPARTS, B * D, S], BF16, kind="Internal").ap()
    scratch_x = nc.dram_tensor("scratch_x", [B * S, D], F32, kind="Internal").ap()
    scratch_o = nc.dram_tensor("scratch_o", [NG, HD + 1, S], F32, kind="Internal").ap()
    scratch_r = nc.dram_tensor("scratch_r", [NG, S], F32, kind="Internal").ap()

    x_rows = a["x"].rearrange("b s d -> (b s) d")
    out_rows = out.rearrange("b s d -> (b s) d")

    top = ExitStack()
    with top:
        def sem(name):
            return top.enter_context(nc.semaphore(name))

        def sems(name, n):
            return [sem(f"{name}{i}") for i in range(n)]

        def allocator(stack):
            def sb(name, shape, dt=F32):
                return stack.enter_context(nc.sbuf_tensor(name, shape, dt))
            return sb

        ident = allocator(top)("ident", [P, P])
        psum = top.enter_context(nc.psum_tensor("psum", [P, NBANK, 512], F32))

        first = ExitStack()
        sb = allocator(first)
        v_all = sb("v_all", [P, NG, KT, HD])
        keep = ExitStack()
        sb = allocator(keep)
        w_qk = sb("w_qk", [P, DT, 2 * D])
        w_v = sb("w_v", [P, DT, D])
        wf_r = sb("wf_r", [P, DT, D])
        wf_k = sb("wf_k", [P, DT, D])
        wf_v = sb("wf_v", [P, DT, D])
        mu = sb("mu", [P, 2, DT])
        b_out = sb("b_out", [P, D])
        cos_t = sb("cos_t", [P, S])
        sin_t = sb("sin_t", [P, S])
        x_in = [sb(f"x_in{c}", [P, TT, D]) for c in range(NC)]
        xn = [sb(f"xn{p}", [P, TT, D]) for p in range(2)]
        xn_t = [sb(f"xn_t{p}", [P, DT, CH + 1]) for p in range(2)]
        x_mix = [sb(f"x_mix{p}", [P, 2, DT, CH]) for p in range(2)]
        x_dif = sb("x_dif", [P, DT, CH])
        r_cos = [sb(f"r_cos{j}", [P, CH]) for j in range(4)]
        r_sin = [sb(f"r_sin{j}", [P, CH]) for j in range(4)]
        parts = [sb(f"parts{j}", [P, NPARTS, CH], BF16) for j in range(4)]
        r_gate = [sb(f"r_gate{i}", [P, 512]) for i in range(2)]
        k_act = sb("k_act", [P, DT, CH])
        stats1 = sb("stats1", [P, TT, 6])
        mv1 = sb("mv1", [P, TT, 2])
        nt1 = sb("nt1", [P, 4, TT])
        keep.close()

        attn = ExitStack()
        sb = allocator(attn)
        NSTK, NP, NST = 3, 4, 3
        q_stk = [sb(f"q_stk{j}", [P, S], BF16) for j in range(NSTK)]
        k_stk = [sb(f"k_stk{j}", [P, S], BF16) for j in range(NSTK)]
        v_head = [sb(f"v_head{j}", [P, KT, 2 * HD]) for j in range(NSTK)]
        probs = [sb(f"probs{n}", [P, S]) for n in range(NP)]
        o_head = [sb(f"o_head{j}", [P, 512]) for j in range(NSTK)]
        max_part = [sb(f"max_part{i}", [P, KT, 4]) for i in range(NSTK)]
        neg_max = sb("neg_max", [P, KT])
        neg_hl = sb("neg_hl", [P, 2, KT], BF16)
        neg_t = [sb(f"neg_t{j}", [P, 32], BF16) for j in range(NSTK)]
        attn.close()
        first.close()

        second = ExitStack()
        sb = allocator(second)
        w_out = sb("w_out", [P, DT, D])
        w2 = {n: sb(f"w2{n}", [P, DT, INNER]) for n in "qkv"}
        w_o2 = sb("w_o2", [P, IT, D])
        wa = {n: sb(f"wa_{n}", [P, DT, D]) for n in ("w", "1", "2")}
        w_12 = sb("w_12", [P, DT, D])
        w_ffn = sb("w_ffn", [P, DT, D])
        col = sb("col", [P, 5, IT])
        half_aug = sb("half_aug", [P, IT])
        decay = sb("decay", [P, IT])
        v_scale = sb("v_scale", [P, IT])
        v_bias = sb("v_bias", [P, IT])
        row_bc = sb("row_bc", [P, 4, D])
        head_sel = sb("head_sel", [P, 32])
        xc = [sb(f"xc{c}", [P, TT, D]) for c in range(NC)]
        a_raw = [sb(f"a_raw{p}", [P, DT, CH]) for p in range(2)]
        a_sum = [sb(f"a_sum{p}", [P, DT, CH]) for p in range(2)]
        xn2 = sb("xn2", [P, TT, D])
        xn2_t = [sb(f"xn2_t{p}", [P, DT, CH]) for p in range(2)]
        recip = sb("recip", [P, NG * S // P])
        q2 = [sb(f"q2{p}", [P, IT, CH]) for p in range(2)]
        qk2 = sb("qk2", [P, IT, CH])
        v2 = sb("v2", [P, IT, CH])
        state = [sb(f"state{p}", [P, IT, CH]) for p in range(2)]
        gate2 = sb("gate2", [P, IT, CH])
        o2 = sb("o2", [P, IT, CH])
        lg = sb("lg", [P, CH])
        aw = sb("aw", [P, TT, H2])
        aw_wide = sb("aw_wide", [P, TT, INNER])
        aw_small = sb("aw_small", [P, 3, TT])
        z2 = sb("z2", [P, TT, D])
        f2 = [sb(f"f2{p}", [P, TT, D]) for p in range(2)]
        stats2 = sb("stats2", [P, TT, 6])
        mv2 = sb("mv2", [P, TT, 2])
        nt2 = sb("nt2", [P, 4, TT])
        second.close()

        consts_in = sem("consts_in")
        full, free = sems("bank_full", NBANK), sems("bank_free", NBANK)
        phase_done = sem("phase_done")
        x_loaded, x_stored = sems("x_loaded", NC), sems("x_stored", NC)
        xn_ready, xnt_ready, dif_ready, mix_ready = (
            sem("xn_ready"), sem("xnt_ready"), sem("dif_ready"), sem("mix_ready"))
        bias_added, x1_ready = sem("bias_added"), sem("x1_ready")
        swap_ready = sem("swap_ready")
        rot_ready, hi_ready, rem_ready, mid_ready, lo_ready = (
            sem("rot_ready"), sem("hi_ready"), sem("rem_ready"), sem("mid_ready"), sem("lo_ready"))
        parts_stored = sems("parts_stored", 4)
        kact_ready, gate_ready = sem("kact_ready"), sem("gate_ready")
        ones_set = sem("ones_set")
        stk_loaded, neg_loaded = sems("stk_loaded", NSTK), sems("neg_loaded", NSTK)
        st_full, st_free = sems("st_full", NST), sems("st_free", NST)
        mx_full, mx_free = sems("mx_full", 4), sems("mx_free", 4)
        pv_done = sems("pv_done", 2)
        po_free = sems("po_free", NSTK)
        v_ready = sem("v_ready")
        shift_stage = sem("shift_stage")
        o_stored = sems("o_stored", NSTK)
        w2_in = sem("w2_in")
        prep, sums_in, recip_ready, recip_out = sem("prep"), sem("sums_in"), sem("recip_ready"), sem("recip_out")
        tanh_alpha = sem("tanh_alpha")
        x1_loaded, heads_loaded, out_stored = sems("x1_loaded", NC), sems("heads_loaded", 2), sems("out_stored", NC)
        at_ready, xn2_ready, xn2t_ready = sem("at_ready"), sem("xn2_ready"), sem("xn2t_ready")
        q2_ready, qk2_ready, v2_ready = sem("q2_ready"), sem("qk2_ready"), sem("v2_ready")
        lg_ready, lgs_ready, ex_ready, aw_ready = (
            sem("lg_ready"), sem("lgs_ready"), sem("ex_ready"), sem("aw_ready"))
        awn_ready = sem("awn_ready")
        state_ready, qs_ready, gate2_ready, o2_ready = (
            sem("state_ready"), sem("qs_ready"), sem("gate2_ready"), sem("o2_ready"))
        z2_ready, fb_ready, f2_ready, y_ready = (
            sem("z2_ready"), sem("fb_ready"), sem("f2_ready"), sem("y_ready"))

        class Ring:
            def __init__(self, start, head, loop, tail, turns):
                assert len(loop) % NBANK == 0
                self.rounds = len(loop) // NBANK
                at_loop = start + len(head)
                at_tail = at_loop + turns * len(loop)
                self.place = {"head": {x: start + k for k, x in enumerate(head)},
                              "loop": {x: at_loop + k for k, x in enumerate(loop)},
                              "tail": {x: at_tail + k for k, x in enumerate(tail)}}
                self.end = at_tail + len(tail)

        TURNS = B - 1

        def step1(c, more):
            return ([("qk", c, j) for j in range(4)] + [("v", c, 0), ("v", c, 1), ("fk", c, 0), ("fk", c, 1),
                    ("r", c, 0), ("r", c, 1)] + [("t", c + 1, 0), ("t", c + 1, 1)] * more
                    + [("fv", c, 0), ("fv", c, 1)])

        SEG1 = {"head": [], "loop": [0, 1, 2, 3], "tail": [0, 1, 2, 3]}
        ring1 = Ring(0, [("t", 0, 0), ("t", 0, 1)], sum((step1(c, True) for c in SEG1["loop"]), []),
                     sum((step1(c, c < 3) for c in SEG1["tail"]), []), TURNS)

        def step3(c, before, more):
            return ([("q", c, j) for j in range(IT)] + [("k", c, j) for j in range(IT)]
                    + [("wo", c - 1, 0), ("wo", c - 1, 1)] * before
                    + [("op", c + 1, 0), ("op", c + 1, 1)] * more
                    + [("lg", c, 0), ("v", c, 0), ("v", c, 1), ("lt", c, 0), ("v", c, 2), ("v", c, 3),
                       ("f", c, 0), ("f", c, 1)]
                    + [("t", c + 1, 0), ("t", c + 1, 1)] * more + [("aw", c, j) for j in range(IT)])

        SEG3 = {"head": [0], "loop": [1, 2, 3, 4], "tail": [1, 2, 3]}
        ring3 = Ring(ring1.end, [("prep", 0, 0), ("prep", 0, 1), ("op", 0, 0), ("op", 0, 1), ("t", 0, 0), ("t", 0, 1)]
                     + step3(0, False, True), sum((step3(c, True, True) for c in SEG3["loop"]), []),
                     sum((step3(c, True, c < 3) for c in SEG3["tail"]), []) + [("wo", 3, 0), ("wo", 3, 1)], TURNS)

        class Banks:

            def __init__(self, eng, ring, segment, turn):
                self.eng, self.place = eng, ring.place[segment]
                self.past = turn * ring.rounds if segment == "loop" else 0

            def claim(self, item):
                k = self.place[item]
                self.eng.wait_ge(free[k % NBANK], self.past + (k // NBANK + OPEN))
                return psum[:, k % NBANK, :]

            def arrived(self, item):
                k = self.place[item]
                self.eng.wait_ge(full[k % NBANK], self.past + (k // NBANK + 1))
                return psum[:, k % NBANK, :]

            def was_read(self, item):
                k = self.place[item]
                self.eng.wait_ge(free[k % NBANK], self.past + (k // NBANK + 1 + OPEN))
                return psum[:, k % NBANK, :]

            def full(self, item):
                return full[self.place[item] % NBANK]

            def free(self, item):
                return free[self.place[item] % NBANK]

        def run_dense(eng, segments, step):
            for c in segments["head"]:
                step("head", 0, c)
            with eng.Fori(0, TURNS) as turn:
                for c in segments["loop"]:
                    step("loop", turn, c)
            for c in segments["tail"]:
                step("tail", TURNS, c)

        def there(segment, c):
            return segment != "tail" or c < NC

        def end_phase(eng, n):
            eng.drain().then_inc(phase_done, 1)
            eng.wait_ge(phase_done, 5 * n)

        AHEAD = 4
        WEIGH_AT = 1

        def max_tile(g_off, s):
            return (g_off + 1, s + AHEAD) if s < KT - AHEAD else (g_off + 2, s + AHEAD - KT)

        LOOP = 20

        def run_heads(eng, head):
            head(0, 0)
            with eng.Fori(0, LOOP) as turn:
                for j in (1, 2, 3):
                    head(turn, j)
            for j in (1, 2, 3):
                head(LOOP, j)

        def score_number(j, kt, c):
            return 4 * (KT * j + kt) + c

        def score_count(turn, n):
            return turn * (3 * 4 * KT // NST) + n // NST

        def exists(turn, j):
            return not isinstance(turn, int) or 3 * turn + j < NG

        block = top.enter_context(nc.Block())

        @block.sync
        def _(sp):
            for room in (*free, *mx_free, *st_free, *pv_done, *po_free, xnt_ready, lo_ready, y_ready, qs_ready):
                sp.sem_inc(room, OPEN)
            for room in (*x_stored, *parts_stored, *o_stored):
                sp.sem_inc(room, OPEN_DMA)
            for dst, src in ((w_qk, a["w_qk"]), (w_v, a["w_v"]), (wf_r, a["wf_r"]),
                             (wf_k, a["wf_k"]), (wf_v, a["wf_v"])):
                sp.dma_start(dst[:, :, :], src.rearrange("(t p) n -> p t n", p=P)).then_inc(consts_in, 16)
            sp.dma_start(mu[:, :, :], a["mu"]).then_inc(consts_in, 16)
            sp.dma_start(b_out[:, :], a["b_out"].partition_broadcast(P)).then_inc(consts_in, 16)
            sp.dma_start(ident[:, :], a["ident"]).then_inc(consts_in, 16)
            sp.dma_start(cos_t[:, :], a["cos"]).then_inc(consts_in, 16)
            sp.dma_start(sin_t[:, :], a["sin"]).then_inc(consts_in, 16)


            def load(turn, c):
                src = x_rows[bass.ds(turn * S + c * CH, CH), :]
                sp.dma_start(x_in[c % NC][:, :, :], src.rearrange("(t p) d -> p t d", p=P)).then_inc(x_loaded[c % NC], 16)

            for c in range(3):
                load(0, c)

            def step(segment, turn, c):
                if there(segment, c + 3):
                    sp.wait_ge(x_stored[(c + 3) % NC], turn * 16 + (16 * (c > 0) + OPEN_DMA))
                    load(turn, c + 3)
                for j in range(4):
                    dst, tile = ((scratch_q, j) if j < 2 else (scratch_k, j - 2))
                    sp.wait_ge(lo_ready, turn * (4 * NC) + (4 * c + j + 1 + OPEN))
                    rows = dst[:, bass.ds(turn * D + tile * P, P), c * CH:(c + 1) * CH]
                    sp.dma_start(rows.rearrange("a p t -> p a t"), parts[j][:, :, :]).then_inc(parts_stored[j], 16)
                sp.wait_ge(x1_ready, turn * NC + (c + 1))
                dst = scratch_x[bass.ds(turn * S + c * CH, CH), :]
                sp.dma_start(dst.rearrange("(t p) d -> p t d", p=P), x_in[c][:, :, :]).then_inc(x_stored[c], 16)

            run_dense(sp, SEG1, step)
            for c in range(NC):
                sp.wait_ge(x_stored[c], 16 * B + OPEN_DMA)
            for j in range(4):
                sp.wait_ge(parts_stored[j], 16 * B * NC + OPEN_DMA)
            end_phase(sp, 1)

            def load_stack(g, j):
                for part0, n, row in ((0, 3, 0), (0, 2, 3 * HD), (0, 1, 5 * HD)):
                    for i in range(n):
                        src = scratch_q[part0 + i, bass.ds(g * HD, HD), :]
                        sp.dma_start(q_stk[j][row + i * HD:row + (i + 1) * HD, :], src).then_inc(stk_loaded[j], 16)
                for part, n, row in ((0, 3, 0), (1, 2, 3 * HD), (2, 1, 5 * HD)):
                    for i in range(n):
                        src = scratch_k[part, bass.ds(g * HD, HD), :]
                        sp.dma_start(k_stk[j][row + i * HD:row + (i + 1) * HD, :], src).then_inc(stk_loaded[j], 16)

            def load_neg(count, j):
                sp.wait_ge(shift_stage, count)
                for quad in range(4):
                    for half in range(2):
                        row = q_stk[j][ROWS + half:ROWS + half + 1, :].rearrange(
                            "p (t q i) -> p q t i", q=4, i=32)[:, quad]
                        base = 32 * quad + KT * half
                        sp.dma_start(row, neg_t[j][base:base + KT, :]).then_inc(neg_loaded[j], 16)

            sp.wait_ge(ones_set, 2)
            for g in range(NSTK):
                load_stack(g, g)
            load_neg(4, 0)

            def store_output(turn, j):
                sp.wait_ge(po_free[j % 3], turn + (j // 3 + 1 + OPEN))
                for c in range(4):
                    dst = scratch_o[bass.ds(turn * 3 + j, 1), :, c * 512:(c + 1) * 512].squeeze(0)
                    sp.dma_start(dst, o_head[j % 3][32 * c:32 * c + HD + 1, :]).then_inc(o_stored[j % 3], 16)

            def head(turn, j):
                if j > 0:
                    store_output(turn, j - 1)
                if exists(turn, j + 1):
                    load_neg(turn * (3 * 4) + 4 * (j + 2), (j + 1) % 3)
                if exists(turn, j + 3):
                    n = score_number(j, KT, 0) - 1
                    sp.wait_ge(st_full[n % NST], score_count(turn, n) + 1)
                    load_stack(turn * 3 + (j + 3), j % 3)

            run_heads(sp, head)
            store_output(LOOP, 3)
            for j in range(3):
                sp.wait_ge(o_stored[j], 64 * (LOOP + 1 + (j == 0)) + OPEN_DMA)
            end_phase(sp, 2)

            for n, name in (("q", "w2_q"), ("k", "w2_k"), ("v", "w2_v")):
                sp.dma_start(w2[n][:, :, :], a[name].rearrange("(t p) n -> p t n", p=P)).then_inc(w2_in, 16)
            for dst, name in ((w_out, "w_out"), (w_o2, "w_o2"), (wa["w"], "wa_w"), (wa["1"], "wa_1"), (wa["2"], "wa_2")):
                sp.dma_start(dst[:, :, :], a[name].rearrange("(t p) n -> p t n", p=P)).then_inc(w2_in, 16)
            sp.dma_start(col[:, :, :], a["col"]).then_inc(w2_in, 16)
            for i, name in enumerate(("bo", "f_bias", "ln_scale", "ln_bias")):
                sp.dma_start(row_bc[:, i, :], a[name].partition_broadcast(P)).then_inc(w2_in, 16)

            def load_x(turn, c):
                src = scratch_x[bass.ds(turn * S + c * CH, CH), :]
                sp.dma_start(xc[c % NC][:, :, :], src.rearrange("(t p) d -> p t d", p=P)).then_inc(x1_loaded[c % NC], 16)

            def load_heads(turn, c):
                for ct in range(DT):
                    g = (turn + c // NC) * H + ct * 8
                    cols = slice(c % NC * CH, (c % NC + 1) * CH)
                    sp.dma_start(a_raw[c % 2][:, ct, :], scratch_o[bass.ds(g, 8), 0:HD, cols]).then_inc(heads_loaded[c % 2], 16)
                    sp.dma_start(a_sum[c % 2][:, ct, :], scratch_r[bass.ds(g, 8), cols].unsqueeze(1)
                                 .to_broadcast([8, HD, CH])).then_inc(heads_loaded[c % 2], 16)

            def store(turn, c):
                sp.wait_ge(y_ready, turn * NC + (c + 1 + OPEN))
                dst = out_rows[bass.ds(turn * S + c * CH, CH), :]
                sp.dma_start(dst.rearrange("(t p) d -> p t d", p=P), xc[c % NC][:, :, :]).then_inc(out_stored[c % NC], 16)

            sp.dma_start(recip[:, :], scratch_o[:, HD, :].rearrange("g (u q) -> g u q", u=2)).then_inc(sums_in, 16)
            for c in range(NC):
                load_x(0, c)
            sp.wait_ge(recip_ready, 1)
            sp.dma_start(scratch_r.rearrange("g (u q) -> g u q", u=2), recip[:, :]).then_inc(recip_out, 16)
            sp.wait_ge(recip_out, 16)
            load_heads(0, 0)
            load_heads(0, 1)
            sp.wait_ge(xn2_ready, 1)
            load_heads(0, 2)

            def step(segment, turn, c):
                if there(segment, c + 3):
                    sp.wait_ge(xn2_ready, turn * NC + (c + 2))
                    load_heads(turn, c + 3)
                if segment != "head":
                    store(turn, c - 1)
                if segment == "loop":
                    sp.wait_ge(out_stored[(c - 1) % NC], turn * 16 + 16)
                    load_x(turn, c + 3)

            run_dense(sp, SEG3, step)
            store(TURNS, NC - 1)
            for c in range(NC):
                sp.wait_ge(out_stored[c], 16 * B)

        @block.tensor
        def _(pe):
            mm = nc.tensor.matmul

            def transposes(banks, item, source, pick):
                dst = banks.claim(item)
                for t in range(TT):
                    last = nc.tensor.transpose(dst[:, t * P:(t + 1) * P], pick(source, t), ident[:, :])
                last.then_inc(banks.full(item), 1)

            def by_channel(banks, item, weights, cols, moving, n_k, offset=0):
                dst = banks.claim(item)
                for kt in range(n_k):
                    last = mm(dst, weights[:, kt, cols], moving[:, kt, offset:offset + CH],
                              start=(kt == 0), stop=(kt == n_k - 1))
                last.then_inc(banks.full(item), 1)

            def by_token(banks, item, pair, stationary, weights, n_k, offset=0):
                dst = banks.claim(item)
                for i in range(2):
                    t0 = offset + (2 * pair + i) * P
                    for kt in range(n_k):
                        last = mm(dst[:, i * D:(i + 1) * D], stationary[:, kt, t0:t0 + P],
                                  weights[:, kt, :], start=(kt == 0), stop=(kt == n_k - 1))
                last.then_inc(banks.full(item), 1)

            pe.wait_ge(consts_in, 10 * 16)

            def xn_transposes(banks, turn, c):
                pe.wait_ge(xn_ready, turn * NC + (c + 1))
                for ct in range(DT):
                    transposes(banks, ("t", c, ct), xn[c % 2],
                               lambda src, t: src[:, t, ct * P:(ct + 1) * P])

            xn_transposes(Banks(pe, ring1, "head", 0), 0, 0)

            def step(segment, turn, c):
                banks, p = Banks(pe, ring1, segment, turn), c % 2
                pe.wait_ge(xnt_ready, turn * NC + (c + 1 + OPEN))
                for j in range(4):
                    by_channel(banks, ("qk", c, j), w_qk, slice(j * P, (j + 1) * P), xn_t[p], DT, 1)
                for pair in range(2):
                    by_token(banks, ("v", c, pair), pair, xn_t[p], w_v, DT, 1)
                pe.wait_ge(mix_ready, turn * NC + (c + 1))
                for j in range(DT):
                    by_channel(banks, ("fk", c, j), wf_k, slice(j * P, (j + 1) * P), x_mix[p][:, 1], DT)
                for pair in range(2):
                    by_token(banks, ("r", c, pair), pair, x_mix[p][:, 0], wf_r, DT)
                if there(segment, c + 1):
                    xn_transposes(banks, turn, c + 1)
                pe.wait_ge(kact_ready, turn * NC + (c + 1))
                for pair in range(2):
                    by_token(banks, ("fv", c, pair), pair, k_act, wf_v, DT)

            run_dense(pe, SEG1, step)
            end_phase(pe, 1)

            for bank in range(NBANK):
                pe.wait_ge(free[bank], (ring1.end - bank + NBANK - 1) // NBANK + OPEN)

            def max_scores(turn, g_off, tile, c):
                j = g_off % 3
                if tile == 0 and c == 0:
                    pe.wait_ge(stk_loaded[j], (turn + g_off // 3) * (12 * 16) + 12 * 16)
                pe.wait_ge(mx_free[c], turn * (3 * KT) + (KT * g_off + tile + OPEN))
                mm(psum[:, NST + c, :], q_stk[j][0:ROWS, tile * P:(tile + 1) * P],
                   k_stk[j][0:ROWS, c * 512:(c + 1) * 512], start=True, stop=True).then_inc(mx_full[c], 1)

            def scores(turn, j, kt, c):
                n = score_number(j, kt, c)
                pe.wait_ge(st_free[n % NST], score_count(turn, n) + OPEN)
                mm(psum[:, n % NST, :], k_stk[j % 3][0:ROWS + 2, kt * P:(kt + 1) * P],
                   q_stk[j % 3][0:ROWS + 2, c * 512:(c + 1) * 512], start=True, stop=True).then_inc(st_full[n % NST], 1)

            def weigh(turn, j, pair):
                end = score_number(j, 2 * pair + 2, 0)
                for n in range(end - NST, end):
                    pe.wait_ge(st_free[n % NST], score_count(turn, n) + (1 + OPEN))
                if pair == 0:
                    pe.wait_ge(v_ready, turn * 3 + (j + 1))
                    pe.wait_ge(po_free[(j - 1) % 3], turn + ((j - 1) // 3 + 1 + OPEN))
                for kt in (2 * pair, 2 * pair + 1):
                    for c in range(4):
                        last = mm(psum[32 * c:32 * c + 32, 7, :], v_head[j % 3][:, kt, :],
                                  probs[kt % NP][:, c * 512:(c + 1) * 512], start=(kt == 0), stop=(kt == KT - 1))
                last.then_inc(pv_done[pair % 2], 1)

            pe.wait_ge(ones_set, 2)
            for tile in range(KT + AHEAD):
                for c in range(4):
                    max_scores(0, tile // KT, tile % KT, c)

            def head(turn, j):
                pe.wait_ge(neg_loaded[j % 3], (turn + j // 3) * 128 + 128)
                for kt in range(KT):
                    g_off, tile = max_tile(j, kt)
                    for c in range(4):
                        if exists(turn, g_off):
                            max_scores(turn, g_off, tile, c)
                        scores(turn, j, kt, c)
                        if c == WEIGH_AT and kt % 2:
                            if kt > 1:
                                weigh(turn, j, kt // 2 - 1)
                            elif j > 0:
                                weigh(turn, j - 1, KT // 2 - 1)

            run_heads(pe, head)
            weigh(LOOP, 3, KT // 2 - 1)
            end_phase(pe, 2)

            pe.wait_ge(w2_in, 13 * 16)
            banks = Banks(pe, ring3, "head", 0)
            for n, (lhs_t, rhs) in enumerate(((wa["1"], wa["2"]), (wa["w"], w_12))):
                dst = banks.claim(("prep", 0, n))
                if n:
                    banks.was_read(("prep", 0, 0))
                for j in range(DT):
                    for kt in range(DT):
                        last = mm(dst[:, j * D:(j + 1) * D], lhs_t[:, kt, j * P:(j + 1) * P],
                                  rhs[:, kt, :], start=(kt == 0), stop=(kt == DT - 1))
                last.then_inc(banks.full(("prep", 0, n)), 1)
            banks.was_read(("prep", 0, 1))
            pe.wait_ge(prep, 1)

            def project_out(banks, turn, c):
                pe.wait_ge(at_ready, turn * NC + (c + 1))
                for pair in range(2):
                    by_token(banks, ("op", c, pair), pair, a_raw[c % 2], w_out, DT)

            def xn_transposes2(banks, turn, c):
                pe.wait_ge(xn2_ready, turn * NC + (c + 1))
                for ct in range(DT):
                    transposes(banks, ("t", c, ct), xn2, lambda src, t: src[:, t, ct * P:(ct + 1) * P])

            def output2(banks, turn, c):
                pe.wait_ge(o2_ready, turn * NC + (c + 1))
                for pair in range(2):
                    by_token(banks, ("wo", c, pair), pair, o2, w_o2, IT)

            def project2(banks, name, c, j):
                by_channel(banks, (name, c, j), w2[name], slice(j * P, (j + 1) * P), xn2_t[c % 2], DT)

            project_out(banks, 0, 0)
            xn_transposes2(banks, 0, 0)

            def step(segment, turn, c):
                banks = Banks(pe, ring3, segment, turn)
                pe.wait_ge(xn2t_ready, turn * NC + (c + 1))
                for name in "qk":
                    for j in range(IT):
                        project2(banks, name, c, j)
                if segment != "head":
                    output2(banks, turn, c - 1)
                if there(segment, c + 1):
                    project_out(banks, turn, c + 1)
                item = ("lg", c, 0)
                pe.wait_ge(qk2_ready, turn * NC + (c + 1))
                dst = banks.claim(item)
                for j in range(IT):
                    last = mm(dst[32 * j:32 * j + 32, :], head_sel[:, :], qk2[:, j, :], start=True, stop=True)
                last.then_inc(banks.full(item), 1)
                project2(banks, "v", c, 0)
                project2(banks, "v", c, 1)
                pe.wait_ge(lg_ready, turn * NC + (c + 1))
                transposes(banks, ("lt", c, 0), lg, lambda src, t: src[:, t * P:(t + 1) * P])
                project2(banks, "v", c, 2)
                project2(banks, "v", c, 3)
                for pair in range(2):
                    by_token(banks, ("f", c, pair), pair, xn2_t[c % 2], w_ffn, DT)
                if there(segment, c + 1):
                    xn_transposes2(banks, turn, c + 1)
                pe.wait_ge(aw_ready, turn * NC + (c + 1))
                for j in range(IT):
                    transposes(banks, ("aw", c, j), aw_wide, lambda src, t: src[:, t, 2 * HD2 * j:2 * HD2 * (j + 1)])

            run_dense(pe, SEG3, step)
            output2(Banks(pe, ring3, "tail", TURNS), TURNS, NC - 1)

        @block.scalar
        def _(act):
            def copy(dst, src):
                return nc.scalar.activation(dst, src, ACT.Copy)

            act.wait_ge(consts_in, 10 * 16)

            def evacuate_t(banks, turn, c):
                p = c % 2
                for ct in range(DT):
                    item = ("t", c, ct)
                    copy(xn_t[p][:, ct, 1:CH + 1], banks.arrived(item)).then_inc(banks.free(item), 1)
                if c % NC == 0:
                    nc.scalar.activation(xn_t[p][:, :, 0:1], ident[:, 0:DT].unsqueeze(2), ACT.Copy, scale=0.0)
                else:
                    act.wait_ge(xnt_ready, turn * NC + (c + OPEN))
                    copy(xn_t[p][:, :, 0:1], xn_t[1 - p][:, :, CH:CH + 1])
                act.drain().then_inc(xnt_ready, 1)

            evacuate_t(Banks(act, ring1, "head", 0), 0, 0)

            def step(segment, turn, c):
                banks = Banks(act, ring1, segment, turn)

                def split_hi(j):
                    act.wait_ge(rot_ready, turn * (4 * NC) + (4 * c + j + 1))
                    act.wait_ge(parts_stored[j], turn * (16 * NC) + (16 * c + OPEN_DMA))
                    copy(parts[j][:, 0, :], r_cos[j][:, :]).then_inc(hi_ready, 1)

                def split_mid(j):
                    act.wait_ge(rem_ready, turn * (4 * NC) + (4 * c + j + 1))
                    copy(parts[j][:, 1, :], r_cos[j][:, :]).then_inc(mid_ready, 1)

                def keep_v(pair):
                    item = ("v", c, pair)
                    src = banks.arrived(item).rearrange("p (t h d) -> p t h d", t=2, h=H)
                    for i in range(2):
                        last = copy(v_all[:, bass.ds(turn * H, H), c * TT + 2 * pair + i, :], src[:, i])
                    last.then_inc(banks.free(item), 1)

                def relu(j):
                    item = ("fk", c, j)
                    nc.scalar.activation(k_act[:, j, :], banks.arrived(item), ACT.Relu).then_inc(banks.free(item), 1)

                def gate(pair):
                    item = ("r", c, pair)
                    nc.scalar.activation(r_gate[pair][:, :], banks.arrived(item), ACT.Tanh, scale=0.5)\
                        .then_inc(banks.free(item), 1)

                split_hi(0)
                split_hi(1)
                split_mid(0)
                keep_v(0)
                keep_v(1)
                split_mid(1)
                split_hi(2)
                relu(0)
                relu(1)
                banks.was_read(("fk", c, 0))
                banks.was_read(("fk", c, 1))
                nc.scalar.activation(k_act[:, :, :], k_act[:, :, :], ACT.Square).then_inc(kact_ready, 1)
                split_hi(3)
                gate(0)
                split_mid(2)
                gate(1)
                act.drain().then_inc(gate_ready, 1)
                split_mid(3)
                if there(segment, c + 1):
                    evacuate_t(banks, turn, c + 1)

            run_dense(act, SEG1, step)
            end_phase(act, 1)

            def exponentials(turn, j, kt, c):
                if c == 0 and kt % 2 == 0:
                    act.wait_ge(pv_done[kt // 2 % 2], turn * (3 * KT // 4) + (j * (KT // 4) + kt // 4 + OPEN))
                n = score_number(j, kt, c)
                act.wait_ge(st_full[n % NST], score_count(turn, n) + 1)
                nc.scalar.activation(probs[kt % NP][:, c * 512:(c + 1) * 512], psum[:, n % NST, :],
                                     ACT.Exp, scale=HD ** -0.5).then_inc(st_free[n % NST], 1)

            def copy_output(turn, j):
                act.wait_ge(o_stored[j % 3], turn * 64 + (64 * (j // 3) + OPEN_DMA))
                act.wait_ge(pv_done[1], turn * (3 * KT // 4) + ((j + 1) * (KT // 4) + OPEN))
                copy(o_head[j % 3][:, :], psum[:, 7, :]).then_inc(po_free[j % 3], 1)

            def head(turn, j):
                for kt in range(KT):
                    if kt == 2 and j > 0:
                        copy_output(turn, j - 1)
                    for c in range(4):
                        exponentials(turn, j, kt, c)

            run_heads(act, head)
            copy_output(LOOP, 3)
            end_phase(act, 2)

            act.wait_ge(w2_in, 13 * 16)
            nc.scalar.activation(decay[:, :], col[:, 3, :], ACT.Tanh, scale=0.5).then_inc(tanh_alpha, 1)
            banks = Banks(act, ring3, "head", 0)
            for n, dst in enumerate((w_12, w_ffn)):
                item = ("prep", 0, n)
                copy(dst[:, :, :], banks.arrived(item).rearrange("p (j n) -> p j n", j=DT)).then_inc(banks.free(item), 1)
            act.wait_ge(prep, 1)

            def evacuate_t2(banks, c):
                for ct in range(DT):
                    item = ("t", c, ct)
                    copy(xn2_t[c % 2][:, ct, :], banks.arrived(item)).then_inc(banks.free(item), 1)
                act.drain().then_inc(xn2t_ready, 1)

            evacuate_t2(banks, 0)

            def step(segment, turn, c):
                banks, p = Banks(act, ring3, segment, turn), c % 2
                if segment != "head":
                    act.wait_ge(qs_ready, turn * NC + (c - 1 + OPEN))
                for j in range(IT):
                    item = ("q", c, j)
                    nc.scalar.activation(q2[p][:, j, :], banks.arrived(item), ACT.Identity,
                                         bias=col[:, 0, j:j + 1]).then_inc(banks.free(item), 1)
                act.drain().then_inc(q2_ready, 1)
                if segment != "head":
                    act.wait_ge(o2_ready, turn * NC + c)
                for j in range(IT):
                    last = nc.scalar.activation(gate2[:, j, :], q2[p][:, j, :], ACT.Tanh, scale=half_aug[:, j:j + 1])
                last.then_inc(gate2_ready, 1)
                item = ("lg", c, 0)
                nc.scalar.activation(lg[:, :], banks.arrived(item), ACT.Copy, scale=HD2 ** -0.5).then_inc(banks.free(item), 1)
                act.drain().then_inc(lg_ready, 1)
                for j in range(IT):
                    item = ("v", c, j)
                    nc.scalar.activation(v2[:, j, :], banks.arrived(item), ACT.Identity,
                                         bias=v_bias[:, j:j + 1], scale=v_scale[:, j:j + 1]).then_inc(banks.free(item), 1)
                act.drain().then_inc(v2_ready, 1)
                act.wait_ge(lgs_ready, turn * NC + (c + 1))
                nc.scalar.activation(aw[:, :, :], aw[:, :, :], ACT.Exp).then_inc(ex_ready, 1)
                act.wait_ge(awn_ready, turn * NC + (c + 1))
                nc.scalar.activation(aw_wide[:, :, :].rearrange("p t (h d) -> p t h d", h=H2),
                                     aw[:, :, :].unsqueeze(3).to_broadcast([P, TT, H2, HD2]),
                                     ACT.Copy).then_inc(aw_ready, 1)
                if there(segment, c + 1):
                    evacuate_t2(banks, c + 1)
                act.wait_ge(fb_ready, turn * NC + (c + 1))
                nc.scalar.activation(f2[p][:, :, :], f2[p][:, :, :], ACT.Tanh).then_inc(f2_ready, 1)

            run_dense(act, SEG3, step)

        @block.vector
        def _(dve):
            v = nc.vector

            def rsqrt(var, nt, eps):
                val, y, tmp, half = nt[:, 0], nt[:, 1], nt[:, 2], nt[:, 3]
                v.tensor_scalar(val, var, eps, None, ALU.add)
                dve.drain()
                v.tensor_scalar(y.bitcast(I32), val.bitcast(I32), 1, None, ALU.logical_shift_right)
                v.tensor_scalar(half, val, -0.5, None, ALU.mult)
                dve.drain()
                v.tensor_scalar(y.bitcast(I32), y.bitcast(I32), -1.0, float(RSQRT_SEED), ALU.mult, ALU.add)
                dve.drain()
                for _ in range(3):
                    v.tensor_tensor(tmp, y, y, ALU.mult)
                    dve.drain()
                    v.tensor_tensor(tmp, tmp, half, ALU.mult)
                    dve.drain()
                    v.scalar_tensor_tensor(y, tmp, 1.5, y, ALU.add, ALU.mult)
                    dve.drain()
                return y

            def normalise(src, dst, stats, mv, nt, eps):
                for t in range(TT):
                    v.bn_stats(stats[:, t, :], src[:, t, :])
                dve.drain()
                for t in range(TT):
                    v.bn_aggr(mv[:, t, :], stats[:, t, :])
                dve.drain()
                rstd = rsqrt(mv[:, :, 1], nt, eps)
                for t in range(TT):
                    last = v.tensor_scalar(dst[:, t, :], src[:, t, :], mv[:, t, 0:1], rstd[:, t:t + 1],
                                           ALU.subtract, ALU.mult)
                return last

            swap = [(p ^ (HD // 2)) for p in range(32)]

            dve.wait_ge(consts_in, 10 * 16)

            def norm(turn, c):
                dve.wait_ge(x_loaded[c % NC], (turn + c // NC) * 16 + 16)
                dve.wait_ge(xnt_ready, turn * NC + (max(c - 1, 0) + OPEN))
                normalise(x_in[c % NC], xn[c % 2], stats1, mv1, nt1, EPS1).then_inc(xn_ready, 1)

            def mix(turn, c):
                p = c % 2
                dve.wait_ge(dif_ready, turn * NC + (c + 1))
                for which in (1, 0):
                    for ct in range(DT):
                        last = v.scalar_tensor_tensor(x_mix[p][:, which, ct, :], x_dif[:, ct, :], mu[:, which, ct:ct + 1],
                                                      xn_t[p][:, ct, 0:CH], ALU.mult, ALU.add)
                last.then_inc(mix_ready, 1)

            norm(0, 0)
            mix(0, 0)

            def step(segment, turn, c):
                banks = Banks(dve, ring1, segment, turn)

                def rotate(j):
                    item = ("qk", c, j)
                    src = banks.arrived(item)
                    v.tensor_tensor(r_cos[j][:, :], src, cos_t[:, c * CH:(c + 1) * CH], ALU.mult)
                    v.stream_shuffle(r_sin[j][:, :], src, swap).then_inc(banks.free(item), 1)

                def remainder(j):
                    dve.wait_ge(hi_ready, turn * (4 * NC) + (4 * c + j + 1))
                    v.tensor_tensor(r_cos[j][:, :], r_cos[j][:, :], parts[j][:, 0, :], ALU.subtract).then_inc(rem_ready, 1)

                dve.wait_ge(lo_ready, turn * (4 * NC) + (4 * c + OPEN))
                rotate(0)
                rotate(1)
                rotate(2)
                remainder(0)
                rotate(3)
                remainder(1)
                if there(segment, c + 1):
                    norm(turn, c + 1)
                remainder(2)
                remainder(3)
                dve.wait_ge(gate_ready, turn * NC + (c + 1))
                dve.wait_ge(bias_added, turn * NC + (c + 1))
                for pair in range(2):
                    item = ("fv", c, pair)
                    v.scalar_tensor_tensor(r_gate[pair][:, :], r_gate[pair][:, :], 1.0, banks.arrived(item),
                                           ALU.add, ALU.mult).then_inc(banks.free(item), 1)
                for pair in range(2):
                    dst = x_in[c][:, 2 * pair:2 * pair + 2, :].rearrange("p t d -> p (t d)")
                    banks.was_read(("fv", c, pair))
                    last = v.scalar_tensor_tensor(dst, r_gate[pair][:, :], 0.5, dst, ALU.mult, ALU.add)
                last.then_inc(x1_ready, 1)
                if there(segment, c + 1):
                    mix(turn, c + 1)

            run_dense(dve, SEG1, step)
            end_phase(dve, 1)

            def maxima(turn, g_off, tile, c):
                dve.wait_ge(mx_full[c], turn * (3 * KT) + (KT * g_off + tile + 1))
                v.tensor_reduce(max_part[g_off % 3][:, tile, c:c + 1], psum[:, NST + c, :], AX.X, ALU.max)\
                    .then_inc(mx_free[c], 1)

            def shift_rows(turn, g_off, stage):
                count = turn * (3 * 4) + 4 * g_off + stage
                if stage == 0:
                    for c in range(4):
                        dve.wait_ge(mx_free[c], turn * (3 * KT) + (KT * (g_off + 1) + OPEN))
                    last = v.tensor_reduce(neg_max[:, :], max_part[g_off % 3][:, :, :], AX.X, ALU.max, negate=True)
                else:
                    dve.wait_ge(shift_stage, count)
                if stage == 1:
                    last = v.tensor_copy(neg_hl[:, 0, :], neg_max[:, :])
                elif stage == 2:
                    last = v.tensor_tensor(neg_hl[:, 1, :], neg_max[:, :], neg_hl[:, 0, :], ALU.subtract)
                elif stage == 3:
                    last = v.transpose(neg_t[g_off % 3][:, :], neg_hl[:, :, :].rearrange("p a t -> p (a t)"))
                last.then_inc(shift_stage, 1)

            def tile_maxima(turn, g_off, tile):
                for c in range(4):
                    maxima(turn, g_off, tile, c)
                    if tile == 0 and g_off > 0:
                        shift_rows(turn, g_off - 1, c)

            for tile in range(KT + AHEAD):
                tile_maxima(0, tile // KT, tile % KT)

            def head(turn, j):
                for s in range(KT):
                    g_off, tile = max_tile(j, s)
                    if exists(turn, g_off):
                        tile_maxima(turn, g_off, tile)
                    elif tile == 0:
                        if exists(turn, g_off - 1):
                            for stage in range(4):
                                shift_rows(turn, g_off - 1, stage)

            run_heads(dve, head)
            end_phase(dve, 2)

            dve.wait_ge(sums_in, 16)
            v.reciprocal(recip[:, :], recip[:, :]).then_inc(recip_ready, 1)
            dve.wait_ge(tanh_alpha, 1)
            dve.wait_ge(w2_in, 13 * 16)
            v.memset(head_sel[:, :], 0.0)
            v.tensor_scalar(v_scale[:, :], decay[:, :], -1.0, 1.0, ALU.mult, ALU.add)
            v.tensor_scalar(decay[:, :], decay[:, :], 0.5, 0.5, ALU.mult, ALU.add)
            dve.drain()
            v.memset(head_sel[0:HD2, 0:1], 1.0)
            v.memset(head_sel[HD2:P, 1:2], 1.0)
            v.tensor_scalar(half_aug[:, :], col[:, 4, :], 0.5, None, ALU.mult)
            v.tensor_tensor(v_bias[:, :], v_scale[:, :], col[:, 2, :], ALU.mult)
            dve.drain().then_inc(prep, 1)

            def residual_norm(banks, turn, c):
                dve.wait_ge(x1_loaded[c % NC], (turn + c // NC) * 16 + 16)
                for pair in range(2):
                    item = ("op", c, pair)
                    dst = xc[c % NC][:, 2 * pair:2 * pair + 2, :].rearrange("p t d -> p (t d)")
                    v.tensor_tensor(dst, banks.arrived(item), dst, ALU.add).then_inc(banks.free(item), 1)
                dve.drain()
                if c:
                    dve.wait_ge(xn2t_ready, turn * NC + c)
                normalise(xc[c % NC], xn2, stats2, mv2, nt2, EPS1).then_inc(xn2_ready, 1)

            def take_output(banks, turn, c):
                dve.wait_ge(y_ready, turn * NC + (c + OPEN))
                for pair in range(2):
                    item = ("wo", c, pair)
                    src = banks.arrived(item).rearrange("p (t d) -> p t d", t=2)
                    v.scalar_tensor_tensor(z2[:, 2 * pair:2 * pair + 2, :], src, 0.5,
                                           row_bc[:, 0:1, :].to_broadcast([P, 2, D]),
                                           ALU.mult, ALU.add).then_inc(banks.free(item), 1)

            def output_norm():
                dve.drain()
                normalise(z2, z2, stats2, mv2, nt2, EPS2).then_inc(z2_ready, 1)

            residual_norm(Banks(dve, ring3, "head", 0), 0, 0)

            def step(segment, turn, c):
                banks, p = Banks(dve, ring3, segment, turn), c % 2
                dve.wait_ge(q2_ready, turn * NC + (c + 1))
                for j in range(IT):
                    item = ("k", c, j)
                    v.scalar_tensor_tensor(qk2[:, j, :], banks.arrived(item), col[:, 1, j:j + 1], q2[p][:, j, :],
                                           ALU.add, ALU.mult).then_inc(banks.free(item), 1)
                dve.drain().then_inc(qk2_ready, 1)
                if segment != "head":
                    take_output(banks, turn, c - 1)
                if there(segment, c + 1):
                    residual_norm(banks, turn, c + 1)
                item = ("lt", c, 0)
                src = banks.arrived(item).rearrange("p (t j e) -> p t j e", t=TT, j=IT)[:, :, :, 0:2]
                v.tensor_reduce(aw_small[:, 0, :], src, AX.XY, ALU.max)
                dve.drain()
                for t in range(TT):
                    last = v.tensor_scalar(aw[:, t, :].rearrange("p (j e) -> p j e", e=2), src[:, t],
                                           aw_small[:, 0, t:t + 1], None, ALU.subtract)
                last.then_inc(banks.free(item), 1)
                dve.drain().then_inc(lgs_ready, 1)
                dve.wait_ge(ex_ready, turn * NC + (c + 1))
                v.tensor_reduce(aw_small[:, 1, :], aw[:, :, :], AX.X, ALU.add)
                dve.drain()
                v.reciprocal(aw_small[:, 2, :], aw_small[:, 1, :])
                dve.drain()
                v.tensor_tensor(aw[:, :, :], aw[:, :, :],
                                aw_small[:, 2, :].unsqueeze(2).to_broadcast([P, TT, H2]), ALU.mult).then_inc(awn_ready, 1)
                if segment != "head":
                    dve.wait_ge(y_ready, turn * NC + (c - 1 + OPEN))
                for pair in range(2):
                    item = ("f", c, pair)
                    src = banks.arrived(item).rearrange("p (t d) -> p t d", t=2)
                    v.tensor_tensor(f2[p][:, 2 * pair:2 * pair + 2, :], src,
                                    row_bc[:, 1:2, :].to_broadcast([P, 2, D]), ALU.add).then_inc(banks.free(item), 1)
                dve.drain().then_inc(fb_ready, 1)
                dve.wait_ge(v2_ready, turn * NC + (c + 1))
                for j in range(IT):
                    item = ("aw", c, j)
                    v.tensor_tensor(v2[:, j, :], v2[:, j, :], banks.arrived(item), ALU.mult)\
                        .then_inc(banks.free(item), 1)
                for j in range(IT):
                    banks.was_read(("aw", c, j))
                    start = 0.0 if c % NC == 0 else state[1 - p][:, j, CH - 1:CH]
                    v.tensor_tensor_scan(state[p][:, j, :], decay[:, j:j + 1].to_broadcast([P, CH]), v2[:, j, :],
                                         start, ALU.mult, ALU.add).then_inc(state_ready, 1)
                if segment != "head":
                    output_norm()
                dve.wait_ge(gate2_ready, turn * NC + (c + 1))
                dve.wait_ge(qs_ready, turn * NC + (c + 1 + OPEN))
                v.scalar_tensor_tensor(o2[:, :, :].rearrange("p j t -> p (j t)"),
                                       gate2[:, :, :].rearrange("p j t -> p (j t)"), 1.0,
                                       o2[:, :, :].rearrange("p j t -> p (j t)"),
                                       ALU.add, ALU.add).then_inc(o2_ready, 1)

            run_dense(dve, SEG3, step)
            take_output(Banks(dve, ring3, "tail", TURNS), TURNS, NC - 1)
            output_norm()

        @block.gpsimd
        def _(pool):
            g_ = nc.gpsimd
            pool.wait_ge(consts_in, 10 * 16)

            def difference(turn, c):
                pool.wait_ge(xnt_ready, turn * NC + (c + 1 + OPEN))
                if c:
                    pool.wait_ge(mix_ready, turn * NC + c)
                now, before = xn_t[c % 2][:, :, 1:CH + 1], xn_t[c % 2][:, :, 0:CH]
                g_.tensor_tensor(x_dif[:, :, :], now, before, ALU.subtract).then_inc(dif_ready, 1)

            difference(0, 0)

            def step(segment, turn, c):
                banks = Banks(pool, ring1, segment, turn)

                def rotate(j):
                    banks.was_read(("qk", c, j))
                    g_.tensor_tensor(r_sin[j][:, :], r_sin[j][:, :], sin_t[:, c * CH:(c + 1) * CH], ALU.mult)
                    pool.drain()
                    g_.tensor_tensor(r_cos[j][:, :], r_cos[j][:, :], r_sin[j][:, :], ALU.add).then_inc(rot_ready, 1)

                def low(j):
                    pool.wait_ge(mid_ready, turn * (4 * NC) + (4 * c + j + 1))
                    g_.tensor_tensor(parts[j][:, 2, :], r_cos[j][:, :], parts[j][:, 1, :], ALU.subtract).then_inc(lo_ready, 1)

                pool.wait_ge(xn_ready, turn * NC + (c + 1))
                g_.tensor_tensor(x_in[c][:, :, :], x_in[c][:, :, :],
                                 b_out[:, :].unsqueeze(1).to_broadcast([P, TT, D]), ALU.add).then_inc(bias_added, 1)
                rotate(0)
                rotate(1)
                low(0)
                rotate(2)
                low(1)
                rotate(3)
                low(2)
                low(3)
                if there(segment, c + 1):
                    difference(turn, c + 1)

            run_dense(pool, SEG1, step)
            end_phase(pool, 1)

            for j in range(NSTK):
                g_.memset(k_stk[j][ROWS:ROWS + 2, :], 1.0)
            pool.drain().then_inc(ones_set, 1)
            for j in range(NSTK):
                g_.memset(v_head[j][:, :, HD:], 1.0)
            pool.drain().then_inc(ones_set, 1)

            def head(turn, j):
                pool.wait_ge(po_free[j % 3], turn + (j // 3 + OPEN))
                g_.tensor_copy(v_head[j % 3][:, :, 0:HD], v_all[:, bass.ds(turn * 3 + j, 1), :, :].squeeze(1)).then_inc(v_ready, 1)

            run_heads(pool, head)
            end_phase(pool, 2)

            def attention_normal(turn, c):
                pool.wait_ge(heads_loaded[c % 2], turn * 128 + 64 * (c // 2 + 1))
                g_.tensor_tensor(a_raw[c % 2][:, :, :], a_raw[c % 2][:, :, :], a_sum[c % 2][:, :, :], ALU.mult)\
                    .then_inc(at_ready, 1)

            def finish(turn, c):
                xp = xc[c % NC]
                pool.wait_ge(f2_ready, turn * NC + (c + 1))
                g_.tensor_tensor(xp[:, :, :], xp[:, :, :], f2[c % 2][:, :, :], ALU.add)
                pool.wait_ge(z2_ready, turn * NC + (c + 1))
                g_.tensor_tensor(z2[:, :, :], z2[:, :, :], row_bc[:, 2:3, :].to_broadcast([P, TT, D]), ALU.mult)
                pool.drain()
                g_.tensor_tensor(z2[:, :, :], z2[:, :, :], row_bc[:, 3:4, :].to_broadcast([P, TT, D]), ALU.add)
                pool.drain()
                g_.tensor_tensor(xp[:, :, :], xp[:, :, :], z2[:, :, :], ALU.add).then_inc(y_ready, 1)

            attention_normal(0, 0)
            attention_normal(0, 1)

            def step(segment, turn, c):
                for j in range(IT):
                    pool.wait_ge(state_ready, turn * (IT * NC) + (IT * c + j + 1))
                    last = g_.tensor_tensor(o2[:, j, :], q2[c % 2][:, j, :], state[c % 2][:, j, :], ALU.mult)
                last.then_inc(qs_ready, 1)
                if there(segment, c + 2):
                    attention_normal(turn, c + 2)
                if segment != "head":
                    finish(turn, c - 1)

            run_dense(pool, SEG3, step)
            finish(TURNS, NC - 1)


def kernel(**inputs):
    import concourse.bacc as bacc
    from concourse.bass_utils import run_bass_kernel_spmd

    i = {k: np.asarray(x) for k, x in inputs.items()}
    order = np.concatenate([h * HD + np.concatenate([np.arange(0, HD, 2), np.arange(1, HD, 2)]) for h in range(H)])
    w = i["L0_attn_w_qkv"]

    def columns(*names):
        return np.stack([i[n].reshape(-1, P).T for n in names], axis=1)

    inv_freq = (1.0 / np.float32(10000.0) ** (np.arange(0, HD, 2, dtype=np.float32) / np.float32(HD))).astype(np.float32)
    angle = np.outer(np.arange(S, dtype=np.float32), inv_freq).astype(np.float32)
    row = np.arange(P) % HD
    cos = np.cos(angle).T[row % (HD // 2)]
    sin = np.sin(angle).T[row % (HD // 2)] * np.where(row < HD // 2, -1, 1)[:, None]
    arrays = {
        "x": i["L0_attn_x"],
        "w_qk": np.concatenate([w[0:D][order], w[D:2 * D][order]]).T,
        "w_v": w[2 * D:].T, "w_out": i["L0_attn_w_out"].T, "b_out": i["L0_attn_b_out"],
        "wf_r": i["L0_ffn_W_r"].T, "wf_k": i["L0_ffn_W_k"].T, "wf_v": i["L0_ffn_W_v"].T,
        "mu": columns("L0_ffn_mu_r", "L0_ffn_mu_k"),
        "cos": cos.astype(np.float32), "sin": sin.astype(np.float32), "ident": np.eye(P, dtype=np.float32),
        "w2_q": i["L1_attn_Wq"], "w2_k": i["L1_attn_Wk"], "w2_v": i["L1_attn_Wv"], "w_o2": i["L1_attn_Wo"],
        "col": columns("L1_attn_bq", "L1_attn_bk", "L1_attn_bv", "L1_attn_alpha", "L1_attn_aug_param"),
        "bo": i["L1_attn_bo"],
        "ln_scale": i["L1_attn_ln_scale"], "ln_bias": i["L1_attn_ln_bias"],
        "wa_w": i["L1_ffn_weight"].T, "wa_1": i["L1_ffn_aux_weight1"].T, "wa_2": i["L1_ffn_aux_weight2"],
        "f_bias": i["L1_ffn_bias"],
    }
    arrays = {k: np.ascontiguousarray(x) for k, x in arrays.items()}
    nc = bacc.Bacc("TRN2", target_bir_lowering=False, num_devices=1)
    aps = {k: nc.dram_tensor(f"in_{k}", x.shape, mybir.dt.from_np(x.dtype), kind="ExternalInput").ap()
           for k, x in arrays.items()}
    out = nc.dram_tensor("out_x", (B, S, D), F32, kind="ExternalOutput").ap()
    build(nc, aps, out)
    r = run_bass_kernel_spmd(nc, [{f"in_{k}": x for k, x in arrays.items()}], core_ids=[0])
    return r.results[0]["out_x"]
```

```python
import numpy as np
from contextlib import ExitStack

import concourse.bass as bass
from concourse import mybir

F32 = mybir.dt.float32
F32R = mybir.dt.float32r
BF16 = mybir.dt.bfloat16
I32 = mybir.dt.int32
ALU = mybir.AluOpType
ACT = mybir.ActivationFunctionType
AX = mybir.AxisListType

P = 128
B, S, D = 4, 2048, 256
H, HD = 16, 16
NG = B * H
CH = 512
NC = S // CH
TT = CH // P
KT = S // P
DT = D // P
INNER = 512
H2, HD2 = 8, 64
IT = INNER // P
EPS1, EPS2 = 1e-5, 1e-6
NPARTS = 3
ROWS = 6 * HD
NBANK = 8
RSQRT_SEED = 0x5F3759DF
OPEN, OPEN_DMA = 1, 16


def build(nc, a, out):
    scratch_q = nc.dram_tensor("scratch_q", [NPARTS, B * D, S], BF16, kind="Internal").ap()
    scratch_k = nc.dram_tensor("scratch_k", [NPARTS, B * D, S], BF16, kind="Internal").ap()
    scratch_x = nc.dram_tensor("scratch_x", [B * S, D], F32, kind="Internal").ap()
    scratch_o = nc.dram_tensor("scratch_o", [NG, HD + 1, S], F32, kind="Internal").ap()
    scratch_r = nc.dram_tensor("scratch_r", [NG, S], F32, kind="Internal").ap()

    x_rows = a["x"].rearrange("b s d -> (b s) d")
    out_rows = out.rearrange("b s d -> (b s) d")

    top = ExitStack()
    with top:
        def sem(name):
            return top.enter_context(nc.semaphore(name))

        def sems(name, n):
            return [sem(f"{name}{i}") for i in range(n)]

        def allocator(stack):
            def sb(name, shape, dt=F32):
                words[stack] = words.get(stack, 0) + int(np.prod(shape[1:])) // (2 if dt == BF16 else 1)
                return stack.enter_context(nc.sbuf_tensor(name, shape, dt))
            return sb

        words = {}

        ident = allocator(top)("ident", [P, P])
        psum = top.enter_context(nc.psum_tensor("psum", [P, NBANK, 512], F32))

        first = ExitStack()
        sb = allocator(first)
        v_all = sb("v_all", [P, NG, KT, HD])
        keep = ExitStack()
        sb = allocator(keep)
        w_qk = sb("w_qk", [P, DT, 2 * D])
        w_v = sb("w_v", [P, DT, D])
        wf_r = sb("wf_r", [P, DT, D])
        wf_k = sb("wf_k", [P, DT, D])
        wf_v = sb("wf_v", [P, DT, D])
        mu = sb("mu", [P, 2, DT])
        b_out = sb("b_out", [P, D])
        cos_t = sb("cos_t", [P, S])
        sin_t = sb("sin_t", [P, S])
        x_in = [sb(f"x_in{c}", [P, TT, D]) for c in range(NC)]
        xn = [sb(f"xn{p}", [P, TT, D]) for p in range(2)]
        xn_t = [sb(f"xn_t{p}", [P, DT, CH + 1]) for p in range(2)]
        x_mix = [sb(f"x_mix{p}", [P, 2, DT, CH]) for p in range(2)]
        x_dif = sb("x_dif", [P, DT, CH])
        r_cos = [sb(f"r_cos{j}", [P, CH]) for j in range(4)]
        r_sin = [sb(f"r_sin{j}", [P, CH]) for j in range(4)]
        parts = [sb(f"parts{j}", [P, NPARTS, CH], BF16) for j in range(4)]
        r_gate = [sb(f"r_gate{i}", [P, 512]) for i in range(2)]
        k_act = sb("k_act", [P, DT, CH])
        stats1 = sb("stats1", [P, TT, 6])
        mv1 = sb("mv1", [P, TT, 2])
        nt1 = sb("nt1", [P, 4, TT])
        keep.close()

        attn = ExitStack()
        sb = allocator(attn)
        NSTK, NP, NST = 3, 4, 3
        q_stk = [sb(f"q_stk{j}", [P, S], BF16) for j in range(NSTK)]
        k_stk = [sb(f"k_stk{j}", [P, S], BF16) for j in range(NSTK)]
        v_head = [sb(f"v_head{j}", [P, KT, 2 * HD]) for j in range(NSTK)]
        probs = [sb(f"probs{n}", [P, S]) for n in range(NP)]
        o_head = [sb(f"o_head{j}", [P, 512]) for j in range(NSTK)]
        max_part = [sb(f"max_part{i}", [P, KT, 4]) for i in range(NSTK)]
        neg_max = sb("neg_max", [P, KT])
        neg_hl = sb("neg_hl", [P, 2, KT], BF16)
        neg_t = [sb(f"neg_t{j}", [P, 32], BF16) for j in range(NSTK)]
        attn.close()
        first.close()

        second = ExitStack()
        sb = allocator(second)
        a_lo = [sb(f"a_lo{p}", [P, DT, CH]) for p in range(2)]
        a_hi = [sb(f"a_hi{p}", [P, DT, CH]) for p in range(2)]
        o2_lo, o2_hi = sb("o2_lo", [P, IT, CH]), sb("o2_hi", [P, IT, CH])
        xc = [sb(f"xc{c}", [P, TT, D]) for c in range(NC)]
        xn2 = sb("xn2", [P, TT, D])
        xn2_hi = [sb(f"xn2_hi{p}", [P, DT, CH]) for p in range(2)]
        xn2_lo = [sb(f"xn2_lo{p}", [P, DT, CH]) for p in range(2)]
        q2 = [sb(f"q2{p}", [P, IT, CH]) for p in range(2)]
        qk2 = sb("qk2", [P, IT, CH])
        v2 = sb("v2", [P, IT, CH])
        state = [sb(f"state{p}", [P, IT, CH]) for p in range(2)]
        lg = sb("lg", [P, CH])
        aw = sb("aw", [P, TT, H2])
        aw_wide = sb("aw_wide", [P, TT, INNER])
        aw_small = sb("aw_small", [P, 3, TT])
        z2 = sb("z2", [P, TT, D])
        f2 = [sb(f"f2{p}", [P, TT, D]) for p in range(2)]
        stats2 = sb("stats2", [P, TT, 6])
        mv2 = sb("mv2", [P, TT, 2])
        nt2 = sb("nt2", [P, 4, TT])
        second.close()
        whole = ExitStack()
        sb = allocator(whole)
        a_raw = [sb(f"a_raw{p}", [P, DT, CH]) for p in range(2)]
        a_sum = [sb(f"a_sum{p}", [P, DT, CH]) for p in range(2)]
        o2 = sb("o2", [P, IT, CH])
        gate2 = sb("gate2", [P, IT, CH])
        whole.close()

        above = max(words[first] + words[attn], words[second])
        weight_shapes = {"out": [P, DT, D], "q": [P, DT, INNER], "k": [P, DT, INNER], "v": [P, DT, INNER],
                         "o2": [P, IT, D], "ffn": [P, DT, D]}
        early = ExitStack()
        sb = allocator(early)
        sb("below_parts", [P, above])
        w_lo = {n: sb(f"w_lo_{n}", shape) for n, shape in weight_shapes.items()}
        w_hi = {n: sb(f"w_hi_{n}", shape) for n, shape in weight_shapes.items()}
        wa = sb("wa", [P, 4, DT, D])
        recip = wa[:, :, :, :].rearrange("p m k n -> p (m k n)")[:, 0:NG * S // P]
        last_sums = sb("last_sums", [P, S // P])
        col = sb("col", [P, 5, IT])
        half_aug = sb("half_aug", [P, IT])
        decay = sb("decay", [P, IT])
        v_scale = sb("v_scale", [P, IT])
        v_bias = sb("v_bias", [P, IT])
        row_bc = sb("row_bc", [P, 4, D])
        head_sel = sb("head_sel", [P, 32])
        early.close()
        early_whole = ExitStack()
        sb = allocator(early_whole)
        sb("below_weights", [P, above])
        w_whole = {n: sb(f"w_whole_{n}", shape) for n, shape in weight_shapes.items()}
        early_whole.close()

        ident_in, consts_in, tables_in = sem("ident_in"), sem("consts_in"), sem("tables_in")
        full, free = sems("bank_full", NBANK), sems("bank_free", NBANK)
        phase_done = sem("phase_done")
        x_loaded, x_stored = sems("x_loaded", NC), sems("x_stored", NC)
        xn_ready, xnt_ready, dif_ready, mix_ready = (
            sem("xn_ready"), sem("xnt_ready"), sem("dif_ready"), sem("mix_ready"))
        bias_added, x1_ready = sem("bias_added"), sem("x1_ready")
        rot_ready, hi_ready, rem_ready, mid_ready, lo_ready = (
            sem("rot_ready"), sem("hi_ready"), sem("rem_ready"), sem("mid_ready"), sem("lo_ready"))
        parts_stored = sems("parts_stored", 4)
        kact_ready, gate_ready = sem("kact_ready"), sem("gate_ready")
        ones_set = sem("ones_set")
        stk_loaded, neg_loaded = sems("stk_loaded", NSTK), sems("neg_loaded", NSTK)
        st_full, st_free = sems("st_full", NST), sems("st_free", NST)
        mx_full, mx_free = sems("mx_full", 4), sems("mx_free", 4)
        pv_done = sems("pv_done", 2)
        po_free = sems("po_free", NSTK)
        v_ready = sem("v_ready")
        shift_stage = sem("shift_stage")
        o_stored = sems("o_stored", NSTK)
        w2_in = sem("w2_in")
        consts2_ready, sums_in, recip_ready, recip_out = (
            sem("consts2_ready"), sem("sums_in"), sem("recip_ready"), sem("recip_out"))
        w12_full, w12_free = sem("w12_full"), sem("w12_free")
        tanh_alpha = sem("tanh_alpha")
        x1_loaded, heads_loaded, out_stored = sems("x1_loaded", NC), sems("heads_loaded", 2), sems("out_stored", NC)
        at_ready, xn2_ready, xn2t_ready = sem("at_ready"), sem("xn2_ready"), sem("xn2t_ready")
        q2_ready, qk2_ready, v2_ready = sem("q2_ready"), sem("qk2_ready"), sem("v2_ready")
        lg_ready, lgs_ready, ex_ready, aw_ready = (
            sem("lg_ready"), sem("lgs_ready"), sem("ex_ready"), sem("aw_ready"))
        awn_ready = sem("awn_ready")
        state_ready, qs_ready, gate2_ready, o2_ready = (
            sem("state_ready"), sem("qs_ready"), sem("gate2_ready"), sem("o2_ready"))
        weight_hi, weights_split = sem("weight_hi"), sem("weights_split")
        at_full, at_hi_ready, o2_hi_ready, xn2_hi_ready = (
            sem("at_full"), sem("at_hi_ready"), sem("o2_hi_ready"), sem("xn2_hi_ready"))
        o2_full = sem("o2_full")
        z2_ready, fb_ready, f2_ready, y_ready = (
            sem("z2_ready"), sem("fb_ready"), sem("f2_ready"), sem("y_ready"))

        class Ring:
            def __init__(self, start, head, loop, tail, turns):
                assert len(loop) % NBANK == 0
                self.rounds = len(loop) // NBANK
                at_loop = start + len(head)
                at_tail = at_loop + turns * len(loop)
                self.place = {"head": {x: start + k for k, x in enumerate(head)},
                              "loop": {x: at_loop + k for k, x in enumerate(loop)},
                              "tail": {x: at_tail + k for k, x in enumerate(tail)}}
                self.end = at_tail + len(tail)

        TURNS = B - 1

        def step1(c, more):
            return ([("qk", c, j) for j in range(4)] + [("v", c, 0), ("v", c, 1), ("fk", c, 0), ("fk", c, 1),
                    ("r", c, 0), ("r", c, 1)] + [("t", c + 1, 0), ("t", c + 1, 1)] * more
                    + [("fv", c, 0), ("fv", c, 1)])

        SEG1 = {"head": [], "loop": [0, 1, 2, 3], "tail": [0, 1, 2, 3]}
        ring1 = Ring(0, [("t", 0, 0), ("t", 0, 1)], sum((step1(c, True) for c in SEG1["loop"]), []),
                     sum((step1(c, c < 3) for c in SEG1["tail"]), []), TURNS)

        def step3(c, before, more):
            return ([("q", c, j) for j in range(IT)] + [("k", c, j) for j in range(IT)]
                    + [("op", c + 1, 0), ("op", c + 1, 1)] * more
                    + [("lg", c, 0), ("v", c, 0), ("v", c, 1), ("lt", c, 0), ("v", c, 2), ("v", c, 3)]
                    + [("wo", c - 1, 0), ("wo", c - 1, 1)] * before + [("f", c, 0), ("f", c, 1)]
                    + [("t", c + 1, 0), ("t", c + 1, 1)] * more + [("aw", c, j) for j in range(IT)])

        SEG3 = {"head": [0, 1], "loop": [2, 3, 4, 5], "tail": [2, 3]}
        ring3 = Ring(ring1.end, [("op", 0, 0), ("op", 0, 1), ("t", 0, 0), ("t", 0, 1)]
                     + step3(0, False, True) + step3(1, True, True), sum((step3(c, True, True) for c in SEG3["loop"]), []),
                     sum((step3(c, True, c < 3) for c in SEG3["tail"]), []) + [("wo", 3, 0), ("wo", 3, 1)], TURNS)

        class Banks:

            def __init__(self, eng, ring, segment, turn):
                self.eng, self.place = eng, ring.place[segment]
                self.past = turn * ring.rounds if segment == "loop" else 0

            def claim(self, item):
                k = self.place[item]
                self.eng.wait_ge(free[k % NBANK], self.past + (k // NBANK + OPEN))
                return psum[:, k % NBANK, :]

            def arrived(self, item):
                k = self.place[item]
                self.eng.wait_ge(full[k % NBANK], self.past + (k // NBANK + 1))
                return psum[:, k % NBANK, :]

            def was_read(self, item):
                k = self.place[item]
                self.eng.wait_ge(free[k % NBANK], self.past + (k // NBANK + 1 + OPEN))
                return psum[:, k % NBANK, :]

            def full(self, item):
                return full[self.place[item] % NBANK]

            def free(self, item):
                return free[self.place[item] % NBANK]

        def run_dense(eng, segments, step):
            for c in segments["head"]:
                step("head", 0, c)
            with eng.Fori(0, TURNS) as turn:
                for c in segments["loop"]:
                    step("loop", turn, c)
            for c in segments["tail"]:
                step("tail", TURNS, c)

        def there(segment, c):
            return segment != "tail" or c < NC

        def end_phase(eng, n):
            eng.drain().then_inc(phase_done, 1)
            eng.wait_ge(phase_done, 5 * n)

        AHEAD = 4
        WEIGH_AT = 1

        def max_tile(g_off, s):
            return (g_off + 1, s + AHEAD) if s < KT - AHEAD else (g_off + 2, s + AHEAD - KT)

        LOOP = 20

        def run_heads(eng, head):
            head(0, 0)
            with eng.Fori(0, LOOP) as turn:
                for j in (1, 2, 3):
                    head(turn, j)
            for j in (1, 2, 3):
                head(LOOP, j)

        def score_number(j, kt, c):
            return 4 * (KT * j + kt) + c

        def score_count(turn, n):
            return turn * (3 * 4 * KT // NST) + n // NST

        def exists(turn, j):
            return not isinstance(turn, int) or 3 * turn + j < NG

        block = top.enter_context(nc.Block())

        @block.sync
        def _(sp):
            for room in (*free, *mx_free, *st_free, *pv_done, *po_free, xnt_ready, lo_ready, y_ready, qs_ready):
                sp.sem_inc(room, OPEN)
            for room in (*x_stored, *parts_stored, *o_stored):
                sp.sem_inc(room, OPEN_DMA)
            def load(turn, c):
                src = x_rows[bass.ds(turn * S + c * CH, CH), :]
                sp.dma_start(x_in[c % NC][:, :, :], src.rearrange("(t p) d -> p t d", p=P)).then_inc(x_loaded[c % NC], 16)

            def load_weight(dst, name):
                sp.dma_start(dst[:, :, :], a[name].rearrange("(t p) n -> p t n", p=P)).then_inc(consts_in, 16)

            load(0, 0)
            sp.dma_start(ident[:, :], a["ident"]).then_inc(ident_in, 16)
            load_weight(w_qk, "w_qk")
            load_weight(w_v, "w_v")
            sp.dma_start(mu[:, :, :], a["mu"]).then_inc(consts_in, 16)
            load_weight(wf_k, "wf_k")
            load_weight(wf_r, "wf_r")
            sp.dma_start(cos_t[:, :], a["cos"]).then_inc(tables_in, 16)
            sp.dma_start(sin_t[:, :], a["sin"]).then_inc(tables_in, 16)
            load(0, 1)
            sp.dma_start(b_out[:, :], a["b_out"].partition_broadcast(P)).then_inc(tables_in, 16)
            load_weight(wf_v, "wf_v")
            load(0, 2)

            def step(segment, turn, c):
                if there(segment, c + 3):
                    sp.wait_ge(x_stored[(c + 3) % NC], turn * 16 + (16 * (c > 0) + OPEN_DMA))
                    load(turn, c + 3)
                for j in range(4):
                    dst, tile = ((scratch_q, j) if j < 2 else (scratch_k, j - 2))
                    sp.wait_ge(lo_ready, turn * (4 * NC) + (4 * c + j + 1 + OPEN))
                    rows = dst[:, bass.ds(turn * D + tile * P, P), c * CH:(c + 1) * CH]
                    sp.dma_start(rows.rearrange("a p t -> p a t"), parts[j][:, :, :]).then_inc(parts_stored[j], 16)
                sp.wait_ge(x1_ready, turn * NC + (c + 1))
                dst = scratch_x[bass.ds(turn * S + c * CH, CH), :]
                sp.dma_start(dst.rearrange("(t p) d -> p t d", p=P), x_in[c][:, :, :]).then_inc(x_stored[c], 16)

            run_dense(sp, SEG1, step)
            for c in range(NC):
                sp.wait_ge(x_stored[c], 16 * B + OPEN_DMA)
            for j in range(4):
                sp.wait_ge(parts_stored[j], 16 * B * NC + OPEN_DMA)
            end_phase(sp, 1)

            def load_stack(g, j):
                for part0, n, row in ((0, 3, 0), (0, 2, 3 * HD), (0, 1, 5 * HD)):
                    for i in range(n):
                        src = scratch_q[part0 + i, bass.ds(g * HD, HD), :]
                        sp.dma_start(q_stk[j][row + i * HD:row + (i + 1) * HD, :], src).then_inc(stk_loaded[j], 16)
                for part, n, row in ((0, 3, 0), (1, 2, 3 * HD), (2, 1, 5 * HD)):
                    for i in range(n):
                        src = scratch_k[part, bass.ds(g * HD, HD), :]
                        sp.dma_start(k_stk[j][row + i * HD:row + (i + 1) * HD, :], src).then_inc(stk_loaded[j], 16)

            def load_neg(count, j):
                sp.wait_ge(shift_stage, count)
                for quad in range(4):
                    for half in range(2):
                        row = q_stk[j][ROWS + half:ROWS + half + 1, :].rearrange(
                            "p (t q i) -> p q t i", q=4, i=32)[:, quad]
                        base = 32 * quad + KT * half
                        sp.dma_start(row, neg_t[j][base:base + KT, :]).then_inc(neg_loaded[j], 16)

            sp.wait_ge(ones_set, 2)
            for g in range(NSTK):
                load_stack(g, g)
            for dst, name in ((w_whole["out"], "w_out"), (w_whole["q"], "w2_q"), (w_whole["k"], "w2_k"),
                              (w_whole["v"], "w2_v"), (w_whole["o2"], "w_o2"), (wa[:, 0], "wa_w"), (wa[:, 1], "wa_1"), (wa[:, 2], "wa_2")):
                sp.dma_start(dst[:, :, :], a[name].rearrange("(t p) n -> p t n", p=P)).then_inc(w2_in, 16)
            sp.dma_start(col[:, :, :], a["col"]).then_inc(w2_in, 16)
            for i, name in enumerate(("bo", "f_bias", "ln_scale", "ln_bias")):
                sp.dma_start(row_bc[:, i, :], a[name].partition_broadcast(P)).then_inc(w2_in, 16)
            load_neg(4, 0)

            def store_output(turn, j):
                sp.wait_ge(po_free[j % 3], turn + (j // 3 + 1 + OPEN))
                for c in range(4):
                    dst = scratch_o[bass.ds(turn * 3 + j, 1), :, c * 512:(c + 1) * 512].squeeze(0)
                    sp.dma_start(dst, o_head[j % 3][32 * c:32 * c + HD + 1, :]).then_inc(o_stored[j % 3], 16)

            def head(turn, j):
                if j > 0:
                    store_output(turn, j - 1)
                if exists(turn, j + 1):
                    load_neg(turn * (3 * 4) + 4 * (j + 2), (j + 1) % 3)
                if exists(turn, j + 3):
                    n = score_number(j, KT, 0) - 1
                    sp.wait_ge(st_full[n % NST], score_count(turn, n) + 1)
                    load_stack(turn * 3 + (j + 3), j % 3)

            run_heads(sp, head)
            for j in range(3):
                sp.wait_ge(o_stored[j], 64 * (LOOP + 1) + OPEN_DMA)
            sp.wait_ge(weights_split, len(weight_shapes))
            sp.dma_start(recip[0:2 * NG - 2, :],
                         scratch_o[0:NG - 1, HD, :].rearrange("g (u q) -> g u q", u=2)).then_inc(sums_in, 16)
            sp.wait_ge(recip_ready, 1)
            sp.dma_start(scratch_r[0:NG - 1, :].rearrange("g (u q) -> g u q", u=2), recip[0:2 * NG - 2, :])\
                .then_inc(recip_out, 16)
            store_output(LOOP, 3)
            sp.wait_ge(o_stored[0], 64 * (LOOP + 2) + OPEN_DMA)
            end_phase(sp, 2)

            def load_x(turn, c):
                src = scratch_x[bass.ds(turn * S + c * CH, CH), :]
                sp.dma_start(xc[c % NC][:, :, :], src.rearrange("(t p) d -> p t d", p=P)).then_inc(x1_loaded[c % NC], 16)

            def load_heads(turn, c):
                for ct in range(DT):
                    g = (turn + c // NC) * H + ct * 8
                    cols = slice(c % NC * CH, (c % NC + 1) * CH)
                    sp.dma_start(a_raw[c % 2][:, ct, :], scratch_o[bass.ds(g, 8), 0:HD, cols]).then_inc(heads_loaded[c % 2], 16)
                    sp.dma_start(a_sum[c % 2][:, ct, :], scratch_r[bass.ds(g, 8), cols].unsqueeze(1)
                                 .to_broadcast([8, HD, CH])).then_inc(heads_loaded[c % 2], 16)

            def store(turn, c):
                sp.wait_ge(y_ready, turn * NC + (c + 1 + OPEN))
                dst = out_rows[bass.ds(turn * S + c * CH, CH), :]
                sp.dma_start(dst.rearrange("(t p) d -> p t d", p=P), xc[c % NC][:, :, :]).then_inc(out_stored[c % NC], 16)

            sp.wait_ge(recip_out, 16)
            load_heads(0, 0)
            load_x(0, 0)
            load_heads(0, 1)
            for c in range(1, NC):
                load_x(0, c)
            last_row = scratch_r[NG - 1:NG, :].rearrange("g (p q) -> (g p) q", p=P)
            sp.dma_start(last_sums[:, :], scratch_o[NG - 1:NG, HD, :].rearrange("g (p q) -> (g p) q", p=P))\
                .then_inc(sums_in, 16)
            sp.wait_ge(recip_ready, 2)
            sp.dma_start(last_row, last_sums[:, :]).then_inc(recip_out, 16)
            sp.wait_ge(recip_out, 32)

            def step(segment, turn, c):
                if there(segment, c + 2):
                    sp.wait_ge(xn2_ready, turn * NC + (c + 1))
                    load_heads(turn, c + 2)
                if c >= 2:
                    store(turn, c - 2)
                    if there(segment, c + 2):
                        sp.wait_ge(out_stored[(c - 2) % NC], (turn + (c - 2) // NC) * 16 + 16)
                        load_x(turn, c + 2)

            run_dense(sp, SEG3, step)
            store(TURNS, NC - 2)
            store(TURNS, NC - 1)
            for c in range(NC):
                sp.wait_ge(out_stored[c], 16 * B)

        @block.tensor
        def _(pe):
            mm = nc.tensor.matmul

            def transposes(banks, item, source, pick):
                dst = banks.claim(item)
                for t in range(TT):
                    last = nc.tensor.transpose(dst[:, t * P:(t + 1) * P], pick(source, t), ident[:, :])
                last.then_inc(banks.full(item), 1)

            def by_channel(banks, item, weights, cols, moving, n_k, offset=0):
                dst = banks.claim(item)
                for kt in range(n_k):
                    last = mm(dst, weights[:, kt, cols], moving[:, kt, offset:offset + CH],
                              start=(kt == 0), stop=(kt == n_k - 1))
                last.then_inc(banks.full(item), 1)

            def by_token(banks, item, pair, stationary, weights, n_k, offset=0):
                dst = banks.claim(item)
                for i in range(2):
                    t0 = offset + (2 * pair + i) * P
                    for kt in range(n_k):
                        last = mm(dst[:, i * D:(i + 1) * D], stationary[:, kt, t0:t0 + P],
                                  weights[:, kt, :], start=(kt == 0), stop=(kt == n_k - 1))
                last.then_inc(banks.full(item), 1)

            def by_parts(dst, stationary, moving, n_k):
                pairs = [(i, k, m) for k in range(n_k) for i, m in ((0, 0), (0, 1), (1, 0))]
                for n, (i, k, m) in enumerate(pairs):
                    last = mm(dst, stationary(i, k).bitcast(F32R), moving(m, k).bitcast(F32R),
                              start=(n == 0), stop=(n == len(pairs) - 1))
                return last

            def by_channel2(banks, item, name, j, moving, n_k):
                w = (w_hi[name], w_lo[name])
                by_parts(banks.claim(item), lambda i, k: w[i][:, k, j * P:(j + 1) * P],
                         lambda m, k: moving[m][:, k, :], n_k).then_inc(banks.full(item), 1)

            def by_token2(banks, item, pair, stationary, name, n_k):
                w, dst = (w_hi[name], w_lo[name]), banks.claim(item)
                for i in range(2):
                    t0 = (2 * pair + i) * P
                    last = by_parts(dst[:, i * D:(i + 1) * D], lambda m, k: stationary[m][:, k, t0:t0 + P],
                                    lambda m, k: w[m][:, k, :], n_k)
                last.then_inc(banks.full(item), 1)

            pe.wait_ge(ident_in, 16)

            def xn_transposes(banks, turn, c):
                pe.wait_ge(xn_ready, turn * NC + (c + 1))
                for ct in range(DT):
                    transposes(banks, ("t", c, ct), xn[c % 2],
                               lambda src, t: src[:, t, ct * P:(ct + 1) * P])

            xn_transposes(Banks(pe, ring1, "head", 0), 0, 0)
            pe.wait_ge(consts_in, 6 * 16)

            def step(segment, turn, c):
                banks, p = Banks(pe, ring1, segment, turn), c % 2
                pe.wait_ge(xnt_ready, turn * NC + (c + 1 + OPEN))
                for j in range(4):
                    by_channel(banks, ("qk", c, j), w_qk, slice(j * P, (j + 1) * P), xn_t[p], DT, 1)
                for pair in range(2):
                    by_token(banks, ("v", c, pair), pair, xn_t[p], w_v, DT, 1)
                pe.wait_ge(mix_ready, turn * NC + (c + 1))
                for j in range(DT):
                    by_channel(banks, ("fk", c, j), wf_k, slice(j * P, (j + 1) * P), x_mix[p][:, 1], DT)
                for pair in range(2):
                    by_token(banks, ("r", c, pair), pair, x_mix[p][:, 0], wf_r, DT)
                if there(segment, c + 1):
                    xn_transposes(banks, turn, c + 1)
                pe.wait_ge(kact_ready, turn * NC + (c + 1))
                for pair in range(2):
                    by_token(banks, ("fv", c, pair), pair, k_act, wf_v, DT)

            run_dense(pe, SEG1, step)
            end_phase(pe, 1)

            for bank in range(NBANK):
                pe.wait_ge(free[bank], (ring1.end - bank + NBANK - 1) // NBANK + OPEN)

            def max_scores(turn, g_off, tile, c):
                j = g_off % 3
                if tile == 0 and c == 0:
                    pe.wait_ge(stk_loaded[j], (turn + g_off // 3) * (12 * 16) + 12 * 16)
                pe.wait_ge(mx_free[c], turn * (3 * KT) + (KT * g_off + tile + OPEN))
                mm(psum[:, NST + c, :], q_stk[j][0:ROWS, tile * P:(tile + 1) * P],
                   k_stk[j][0:ROWS, c * 512:(c + 1) * 512], start=True, stop=True).then_inc(mx_full[c], 1)

            def scores(turn, j, kt, c):
                n = score_number(j, kt, c)
                pe.wait_ge(st_free[n % NST], score_count(turn, n) + OPEN)
                mm(psum[:, n % NST, :], k_stk[j % 3][0:ROWS + 2, kt * P:(kt + 1) * P],
                   q_stk[j % 3][0:ROWS + 2, c * 512:(c + 1) * 512], start=True, stop=True).then_inc(st_full[n % NST], 1)

            def weigh(turn, j, pair):
                end = score_number(j, 2 * pair + 2, 0)
                for n in range(end - NST, end):
                    pe.wait_ge(st_free[n % NST], score_count(turn, n) + (1 + OPEN))
                if pair == 0:
                    pe.wait_ge(v_ready, turn * 3 + (j + 1))
                    pe.wait_ge(po_free[(j - 1) % 3], turn + ((j - 1) // 3 + 1 + OPEN))
                for kt in (2 * pair, 2 * pair + 1):
                    for c in range(4):
                        last = mm(psum[32 * c:32 * c + 32, 7, :], v_head[j % 3][:, kt, :],
                                  probs[kt % NP][:, c * 512:(c + 1) * 512], start=(kt == 0), stop=(kt == KT - 1))
                last.then_inc(pv_done[pair % 2], 1)

            def merge_weights(n):
                if n == 0:
                    pe.wait_ge(w2_in, 13 * 16)
                else:
                    pe.wait_ge(w12_free, 1)
                lhs_t, rhs = ((1, 2), (0, 3))[n]
                for j in range(DT):
                    for kt in range(DT):
                        last = mm(psum[:, 7, j * D:(j + 1) * D], wa[:, lhs_t, kt, j * P:(j + 1) * P],
                                  wa[:, rhs, kt, :], start=(kt == 0), stop=(kt == DT - 1))
                last.then_inc(w12_full, 1)

            pe.wait_ge(ones_set, 2)
            for tile in range(KT + AHEAD):
                for c in range(4):
                    max_scores(0, tile // KT, tile % KT, c)
                if tile in (KT - 4, KT - 2):
                    merge_weights((tile - (KT - 4)) // 2)
            pe.wait_ge(w12_free, 2)

            def head(turn, j):
                pe.wait_ge(neg_loaded[j % 3], (turn + j // 3) * 128 + 128)
                for kt in range(KT):
                    g_off, tile = max_tile(j, kt)
                    for c in range(4):
                        if exists(turn, g_off):
                            max_scores(turn, g_off, tile, c)
                        scores(turn, j, kt, c)
                        if c == WEIGH_AT and kt % 2:
                            if kt > 1:
                                weigh(turn, j, kt // 2 - 1)
                            elif j > 0:
                                weigh(turn, j - 1, KT // 2 - 1)

            run_heads(pe, head)
            weigh(LOOP, 3, KT // 2 - 1)
            end_phase(pe, 2)

            banks = Banks(pe, ring3, "head", 0)
            pe.wait_ge(weights_split, len(weight_shapes))
            pe.wait_ge(consts2_ready, 1)

            def project_out(banks, turn, c):
                pe.wait_ge(at_ready, turn * NC + (c + 1))
                for pair in range(2):
                    by_token2(banks, ("op", c, pair), pair, (a_hi[c % 2], a_lo[c % 2]), "out", DT)

            def xn_transposes2(banks, turn, c):
                pe.wait_ge(xn2_ready, turn * NC + (c + 1))
                for ct in range(DT):
                    transposes(banks, ("t", c, ct), xn2, lambda src, t: src[:, t, ct * P:(ct + 1) * P])

            def output2(banks, turn, c):
                pe.wait_ge(o2_ready, turn * NC + (c + 1))
                for pair in range(2):
                    by_token2(banks, ("wo", c, pair), pair, (o2_hi, o2_lo), "o2", IT)

            def project2(banks, name, c, j):
                by_channel2(banks, (name, c, j), name, j, (xn2_hi[c % 2], xn2_lo[c % 2]), DT)

            project_out(banks, 0, 0)
            xn_transposes2(banks, 0, 0)

            def step(segment, turn, c):
                banks = Banks(pe, ring3, segment, turn)
                pe.wait_ge(xn2t_ready, turn * NC + (c + 1))
                for name in "qk":
                    for j in range(IT):
                        project2(banks, name, c, j)
                if there(segment, c + 1):
                    project_out(banks, turn, c + 1)
                item = ("lg", c, 0)
                pe.wait_ge(qk2_ready, turn * NC + (c + 1))
                dst = banks.claim(item)
                for j in range(IT):
                    last = mm(dst[32 * j:32 * j + 32, :], head_sel[:, :], qk2[:, j, :], start=True, stop=True)
                last.then_inc(banks.full(item), 1)
                project2(banks, "v", c, 0)
                project2(banks, "v", c, 1)
                pe.wait_ge(lg_ready, turn * NC + (c + 1))
                transposes(banks, ("lt", c, 0), lg, lambda src, t: src[:, t * P:(t + 1) * P])
                project2(banks, "v", c, 2)
                project2(banks, "v", c, 3)
                if c >= 1:
                    output2(banks, turn, c - 1)
                for pair in range(2):
                    by_token2(banks, ("f", c, pair), pair, (xn2_hi[c % 2], xn2_lo[c % 2]), "ffn", DT)
                if there(segment, c + 1):
                    xn_transposes2(banks, turn, c + 1)
                pe.wait_ge(aw_ready, turn * NC + (c + 1))
                for j in range(IT):
                    transposes(banks, ("aw", c, j), aw_wide, lambda src, t: src[:, t, 2 * HD2 * j:2 * HD2 * (j + 1)])

            run_dense(pe, SEG3, step)
            output2(Banks(pe, ring3, "tail", TURNS), TURNS, NC - 1)

        @block.scalar
        def _(act):
            def copy(dst, src):
                return nc.scalar.activation(dst, src, ACT.Copy)

            act.wait_ge(ident_in, 16)

            def evacuate_t(banks, turn, c):
                p = c % 2
                for ct in range(DT):
                    item = ("t", c, ct)
                    copy(xn_t[p][:, ct, 1:CH + 1], banks.arrived(item)).then_inc(banks.free(item), 1)
                if c % NC == 0:
                    nc.scalar.activation(xn_t[p][:, :, 0:1], ident[:, 0:DT].unsqueeze(2), ACT.Copy, scale=0.0)
                else:
                    act.wait_ge(xnt_ready, turn * NC + (c + OPEN))
                    copy(xn_t[p][:, :, 0:1], xn_t[1 - p][:, :, CH:CH + 1])
                act.drain().then_inc(xnt_ready, 1)

            evacuate_t(Banks(act, ring1, "head", 0), 0, 0)

            def step(segment, turn, c):
                banks = Banks(act, ring1, segment, turn)

                def split_hi(j):
                    act.wait_ge(rot_ready, turn * (4 * NC) + (4 * c + j + 1))
                    act.wait_ge(parts_stored[j], turn * (16 * NC) + (16 * c + OPEN_DMA))
                    copy(parts[j][:, 0, :], r_cos[j][:, :]).then_inc(hi_ready, 1)

                def split_mid(j):
                    act.wait_ge(rem_ready, turn * (4 * NC) + (4 * c + j + 1))
                    copy(parts[j][:, 1, :], r_cos[j][:, :]).then_inc(mid_ready, 1)

                def keep_v(pair):
                    item = ("v", c, pair)
                    src = banks.arrived(item).rearrange("p (t h d) -> p t h d", t=2, h=H)
                    for i in range(2):
                        last = copy(v_all[:, bass.ds(turn * H, H), c * TT + 2 * pair + i, :], src[:, i])
                    last.then_inc(banks.free(item), 1)

                def relu(j):
                    item = ("fk", c, j)
                    nc.scalar.activation(k_act[:, j, :], banks.arrived(item), ACT.Relu).then_inc(banks.free(item), 1)

                def gate(pair):
                    item = ("r", c, pair)
                    nc.scalar.activation(r_gate[pair][:, :], banks.arrived(item), ACT.Tanh, scale=0.5)\
                        .then_inc(banks.free(item), 1)

                split_hi(0)
                split_hi(1)
                split_mid(0)
                keep_v(0)
                keep_v(1)
                split_mid(1)
                relu(0)
                relu(1)
                banks.was_read(("fk", c, 0))
                banks.was_read(("fk", c, 1))
                nc.scalar.activation(k_act[:, :, :], k_act[:, :, :], ACT.Square).then_inc(kact_ready, 1)
                split_hi(2)
                split_hi(3)
                gate(0)
                split_mid(2)
                gate(1)
                act.drain().then_inc(gate_ready, 1)
                split_mid(3)
                if there(segment, c + 1):
                    evacuate_t(banks, turn, c + 1)

            run_dense(act, SEG1, step)
            end_phase(act, 1)

            def exponentials(turn, j, kt, c):
                if c == 0 and kt % 2 == 0:
                    act.wait_ge(pv_done[kt // 2 % 2], turn * (3 * KT // 4) + (j * (KT // 4) + kt // 4 + OPEN))
                n = score_number(j, kt, c)
                act.wait_ge(st_full[n % NST], score_count(turn, n) + 1)
                nc.scalar.activation(probs[kt % NP][:, c * 512:(c + 1) * 512], psum[:, n % NST, :],
                                     ACT.Exp, scale=HD ** -0.5).then_inc(st_free[n % NST], 1)

            def copy_output(turn, j):
                act.wait_ge(o_stored[j % 3], turn * 64 + (64 * (j // 3) + OPEN_DMA))
                act.wait_ge(pv_done[1], turn * (3 * KT // 4) + ((j + 1) * (KT // 4) + OPEN))
                copy(o_head[j % 3][:, :], psum[:, 7, :]).then_inc(po_free[j % 3], 1)

            def head(turn, j):
                for kt in range(KT):
                    if kt == 2 and j > 0:
                        copy_output(turn, j - 1)
                    for c in range(4):
                        exponentials(turn, j, kt, c)

            def split_weight(name):
                copy(w_hi[name][:, :, :].bitcast(F32R), w_whole[name][:, :, :]).then_inc(weight_hi, 1)

            act.wait_ge(w2_in, 13 * 16)
            nc.scalar.activation(decay[:, :], col[:, 3, :], ACT.Tanh, scale=0.5).then_inc(tanh_alpha, 1)
            for name in ("out", "q", "k", "v", "o2"):
                split_weight(name)
            for n, dst in enumerate((wa[:, 3], w_whole["ffn"])):
                act.wait_ge(w12_full, n + 1)
                copy(dst[:, :, :], psum[:, 7, :].rearrange("p (j n) -> p j n", j=DT)).then_inc(w12_free, 1)
            act.wait_ge(w12_free, 2)
            split_weight("ffn")

            run_heads(act, head)
            copy_output(LOOP, 3)
            end_phase(act, 2)

            banks = Banks(act, ring3, "head", 0)
            act.wait_ge(consts2_ready, 1)

            def attention_hi(turn, c):
                act.wait_ge(at_full, turn * NC + (c + 1))
                copy(a_hi[c % 2][:, :, :].bitcast(F32R), a_raw[c % 2][:, :, :]).then_inc(at_hi_ready, 1)

            def output_hi(turn, c):
                act.wait_ge(o2_full, turn * NC + (c + 1))
                copy(o2_hi[:, :, :].bitcast(F32R), o2[:, :, :]).then_inc(o2_hi_ready, 1)

            def evacuate_t2(banks, c):
                for ct in range(DT):
                    item = ("t", c, ct)
                    copy(xn2_hi[c % 2][:, ct, :].bitcast(F32R), banks.arrived(item)).then_inc(xn2_hi_ready, 1)

            attention_hi(0, 0)
            evacuate_t2(banks, 0)
            attention_hi(0, 1)

            def step(segment, turn, c):
                banks, p = Banks(act, ring3, segment, turn), c % 2
                if c >= 1:
                    act.wait_ge(qs_ready, turn * NC + (c - 1 + OPEN))
                for j in range(IT):
                    item = ("q", c, j)
                    nc.scalar.activation(q2[p][:, j, :], banks.arrived(item), ACT.Identity,
                                         bias=col[:, 0, j:j + 1]).then_inc(banks.free(item), 1)
                act.drain().then_inc(q2_ready, 1)
                if c >= 1:
                    output_hi(turn, c - 1)
                item = ("lg", c, 0)
                nc.scalar.activation(lg[:, :], banks.arrived(item), ACT.Copy, scale=HD2 ** -0.5).then_inc(banks.free(item), 1)
                act.drain().then_inc(lg_ready, 1)
                for j in range(IT):
                    item = ("v", c, j)
                    nc.scalar.activation(v2[:, j, :], banks.arrived(item), ACT.Identity,
                                         bias=v_bias[:, j:j + 1], scale=v_scale[:, j:j + 1]).then_inc(banks.free(item), 1)
                act.drain().then_inc(v2_ready, 1)
                act.wait_ge(lgs_ready, turn * NC + (c + 1))
                nc.scalar.activation(aw[:, :, :], aw[:, :, :], ACT.Exp).then_inc(ex_ready, 1)
                act.wait_ge(awn_ready, turn * NC + (c + 1))
                nc.scalar.activation(aw_wide[:, :, :].rearrange("p t (h d) -> p t h d", h=H2),
                                     aw[:, :, :].unsqueeze(3).to_broadcast([P, TT, H2, HD2]),
                                     ACT.Copy).then_inc(aw_ready, 1)
                if there(segment, c + 1):
                    evacuate_t2(banks, c + 1)
                act.wait_ge(fb_ready, turn * NC + (c + 1))
                nc.scalar.activation(f2[p][:, :, :], f2[p][:, :, :], ACT.Tanh).then_inc(f2_ready, 1)
                if c >= 1:
                    banks.arrived(("wo", c - 1, 1))
                for j in range(IT):
                    last = nc.scalar.activation(gate2[:, j, :], q2[p][:, j, :], ACT.Tanh, scale=half_aug[:, j:j + 1])
                last.then_inc(gate2_ready, 1)
                if there(segment, c + 2):
                    attention_hi(turn, c + 2)

            run_dense(act, SEG3, step)
            output_hi(TURNS, NC - 1)

        @block.vector
        def _(dve):
            v = nc.vector

            def rsqrt(var, nt, eps):
                val, y, tmp, half = nt[:, 0], nt[:, 1], nt[:, 2], nt[:, 3]
                v.tensor_scalar(val, var, eps, None, ALU.add)
                dve.drain()
                v.tensor_scalar(y.bitcast(I32), val.bitcast(I32), 1, None, ALU.logical_shift_right)
                v.tensor_scalar(half, val, -0.5, None, ALU.mult)
                dve.drain()
                v.tensor_scalar(y.bitcast(I32), y.bitcast(I32), -1.0, float(RSQRT_SEED), ALU.mult, ALU.add)
                dve.drain()
                for _ in range(3):
                    v.tensor_tensor(tmp, y, y, ALU.mult)
                    dve.drain()
                    v.tensor_tensor(tmp, tmp, half, ALU.mult)
                    dve.drain()
                    v.scalar_tensor_tensor(y, tmp, 1.5, y, ALU.add, ALU.mult)
                    dve.drain()
                return y

            def normalise(src, dst, stats, mv, nt, eps):
                for t in range(TT):
                    v.bn_stats(stats[:, t, :], src[:, t, :])
                dve.drain()
                for t in range(TT):
                    v.bn_aggr(mv[:, t, :], stats[:, t, :])
                dve.drain()
                rstd = rsqrt(mv[:, :, 1], nt, eps)
                for t in range(TT):
                    last = v.tensor_scalar(dst[:, t, :], src[:, t, :], mv[:, t, 0:1], rstd[:, t:t + 1],
                                           ALU.subtract, ALU.mult)
                return last

            swap = [(p ^ (HD // 2)) for p in range(32)]


            def norm(turn, c):
                dve.wait_ge(x_loaded[c % NC], (turn + c // NC) * 16 + 16)
                dve.wait_ge(xnt_ready, turn * NC + (max(c - 1, 0) + OPEN))
                normalise(x_in[c % NC], xn[c % 2], stats1, mv1, nt1, EPS1).then_inc(xn_ready, 1)

            def mix(turn, c):
                p = c % 2
                dve.wait_ge(dif_ready, turn * NC + (c + 1))
                for which in (1, 0):
                    for ct in range(DT):
                        last = v.scalar_tensor_tensor(x_mix[p][:, which, ct, :], x_dif[:, ct, :], mu[:, which, ct:ct + 1],
                                                      xn_t[p][:, ct, 0:CH], ALU.mult, ALU.add)
                last.then_inc(mix_ready, 1)

            norm(0, 0)
            dve.wait_ge(consts_in, 6 * 16)
            mix(0, 0)
            dve.wait_ge(tables_in, 3 * 16)

            def step(segment, turn, c):
                banks = Banks(dve, ring1, segment, turn)

                def rotate(j):
                    item = ("qk", c, j)
                    src = banks.arrived(item)
                    v.tensor_tensor(r_cos[j][:, :], src, cos_t[:, c * CH:(c + 1) * CH], ALU.mult)
                    v.stream_shuffle(r_sin[j][:, :], src, swap).then_inc(banks.free(item), 1)

                def remainder(j):
                    dve.wait_ge(hi_ready, turn * (4 * NC) + (4 * c + j + 1))
                    v.tensor_tensor(r_cos[j][:, :], r_cos[j][:, :], parts[j][:, 0, :], ALU.subtract).then_inc(rem_ready, 1)

                dve.wait_ge(lo_ready, turn * (4 * NC) + (4 * c + OPEN))
                rotate(0)
                rotate(1)
                rotate(2)
                remainder(0)
                rotate(3)
                remainder(1)
                if there(segment, c + 1):
                    norm(turn, c + 1)
                remainder(2)
                remainder(3)
                dve.wait_ge(gate_ready, turn * NC + (c + 1))
                dve.wait_ge(bias_added, turn * NC + (c + 1))
                for pair in range(2):
                    item = ("fv", c, pair)
                    v.scalar_tensor_tensor(r_gate[pair][:, :], r_gate[pair][:, :], 1.0, banks.arrived(item),
                                           ALU.add, ALU.mult).then_inc(banks.free(item), 1)
                for pair in range(2):
                    dst = x_in[c][:, 2 * pair:2 * pair + 2, :].rearrange("p t d -> p (t d)")
                    banks.was_read(("fv", c, pair))
                    last = v.scalar_tensor_tensor(dst, r_gate[pair][:, :], 0.5, dst, ALU.mult, ALU.add)
                last.then_inc(x1_ready, 1)
                if there(segment, c + 1):
                    mix(turn, c + 1)

            run_dense(dve, SEG1, step)
            end_phase(dve, 1)

            def maxima(turn, g_off, tile, c):
                dve.wait_ge(mx_full[c], turn * (3 * KT) + (KT * g_off + tile + 1))
                v.tensor_reduce(max_part[g_off % 3][:, tile, c:c + 1], psum[:, NST + c, :], AX.X, ALU.max)\
                    .then_inc(mx_free[c], 1)

            def shift_rows(turn, g_off, stage):
                count = turn * (3 * 4) + 4 * g_off + stage
                if stage == 0:
                    for c in range(4):
                        dve.wait_ge(mx_free[c], turn * (3 * KT) + (KT * (g_off + 1) + OPEN))
                    last = v.tensor_reduce(neg_max[:, :], max_part[g_off % 3][:, :, :], AX.X, ALU.max, negate=True)
                else:
                    dve.wait_ge(shift_stage, count)
                if stage == 1:
                    last = v.tensor_copy(neg_hl[:, 0, :], neg_max[:, :])
                elif stage == 2:
                    last = v.tensor_tensor(neg_hl[:, 1, :], neg_max[:, :], neg_hl[:, 0, :], ALU.subtract)
                elif stage == 3:
                    last = v.transpose(neg_t[g_off % 3][:, :], neg_hl[:, :, :].rearrange("p a t -> p (a t)"))
                last.then_inc(shift_stage, 1)

            def tile_maxima(turn, g_off, tile):
                for c in range(4):
                    maxima(turn, g_off, tile, c)
                    if tile == 0 and g_off > 0:
                        shift_rows(turn, g_off - 1, c)

            for tile in range(KT + AHEAD):
                tile_maxima(0, tile // KT, tile % KT)

            def head(turn, j):
                for s in range(KT):
                    g_off, tile = max_tile(j, s)
                    if exists(turn, g_off):
                        tile_maxima(turn, g_off, tile)
                    elif tile == 0:
                        if exists(turn, g_off - 1):
                            for stage in range(4):
                                shift_rows(turn, g_off - 1, stage)

            run_heads(dve, head)
            dve.wait_ge(tanh_alpha, 1)
            dve.wait_ge(w2_in, 13 * 16)
            v.memset(head_sel[:, :], 0.0)
            v.tensor_scalar(v_scale[:, :], decay[:, :], -1.0, 1.0, ALU.mult, ALU.add)
            v.tensor_scalar(decay[:, :], decay[:, :], 0.5, 0.5, ALU.mult, ALU.add)
            dve.drain()
            v.memset(head_sel[0:HD2, 0:1], 1.0)
            v.memset(head_sel[HD2:P, 1:2], 1.0)
            v.tensor_scalar(half_aug[:, :], col[:, 4, :], 0.5, None, ALU.mult)
            v.tensor_tensor(v_bias[:, :], v_scale[:, :], col[:, 2, :], ALU.mult)
            dve.drain().then_inc(consts2_ready, 1)
            dve.wait_ge(sums_in, 16)
            v.reciprocal(recip[0:2 * NG - 2, :], recip[0:2 * NG - 2, :]).then_inc(recip_ready, 1)
            end_phase(dve, 2)

            def residual_norm(banks, turn, c):
                dve.wait_ge(x1_loaded[c % NC], (turn + c // NC) * 16 + 16)
                for pair in range(2):
                    item = ("op", c, pair)
                    dst = xc[c % NC][:, 2 * pair:2 * pair + 2, :].rearrange("p t d -> p (t d)")
                    v.tensor_tensor(dst, banks.arrived(item), dst, ALU.add).then_inc(banks.free(item), 1)
                dve.drain()
                normalise(xc[c % NC], xn2, stats2, mv2, nt2, EPS1).then_inc(xn2_ready, 1)

            def take_output(banks, turn, c):
                dve.wait_ge(y_ready, turn * NC + (c + OPEN))
                for pair in range(2):
                    item = ("wo", c, pair)
                    src = banks.arrived(item).rearrange("p (t d) -> p t d", t=2)
                    v.scalar_tensor_tensor(z2[:, 2 * pair:2 * pair + 2, :], src, 0.5,
                                           row_bc[:, 0:1, :].to_broadcast([P, 2, D]),
                                           ALU.mult, ALU.add).then_inc(banks.free(item), 1)

            def output_norm():
                dve.drain()
                normalise(z2, z2, stats2, mv2, nt2, EPS2).then_inc(z2_ready, 1)

            def norm_lo(banks, turn, c):
                for ct in range(DT):
                    item = ("t", c, ct)
                    dve.wait_ge(xn2_hi_ready, turn * (DT * NC) + (DT * c + ct + 1))
                    v.tensor_tensor(xn2_lo[c % 2][:, ct, :].bitcast(F32R), banks.arrived(item),
                                    xn2_hi[c % 2][:, ct, :], ALU.subtract).then_inc(banks.free(item), 1)
                dve.drain().then_inc(xn2t_ready, 1)

            residual_norm(Banks(dve, ring3, "head", 0), 0, 0)
            norm_lo(Banks(dve, ring3, "head", 0), 0, 0)
            dve.wait_ge(sums_in, 32)
            v.reciprocal(last_sums[:, :], last_sums[:, :]).then_inc(recip_ready, 1)

            def step(segment, turn, c):
                banks, p = Banks(dve, ring3, segment, turn), c % 2
                dve.wait_ge(q2_ready, turn * NC + (c + 1))
                for j in range(IT):
                    item = ("k", c, j)
                    v.scalar_tensor_tensor(qk2[:, j, :], banks.arrived(item), col[:, 1, j:j + 1], q2[p][:, j, :],
                                           ALU.add, ALU.mult).then_inc(banks.free(item), 1)
                dve.drain().then_inc(qk2_ready, 1)
                if c >= 2:
                    output_norm()
                if there(segment, c + 1):
                    residual_norm(banks, turn, c + 1)
                item = ("lt", c, 0)
                src = banks.arrived(item).rearrange("p (t j e) -> p t j e", t=TT, j=IT)[:, :, :, 0:2]
                v.tensor_reduce(aw_small[:, 0, :], src, AX.XY, ALU.max)
                dve.drain()
                for t in range(TT):
                    last = v.tensor_scalar(aw[:, t, :].rearrange("p (j e) -> p j e", e=2), src[:, t],
                                           aw_small[:, 0, t:t + 1], None, ALU.subtract)
                last.then_inc(banks.free(item), 1)
                dve.drain().then_inc(lgs_ready, 1)
                dve.wait_ge(ex_ready, turn * NC + (c + 1))
                v.tensor_reduce(aw_small[:, 1, :], aw[:, :, :], AX.X, ALU.add)
                dve.drain()
                v.reciprocal(aw_small[:, 2, :], aw_small[:, 1, :])
                dve.drain()
                v.tensor_tensor(aw[:, :, :], aw[:, :, :],
                                aw_small[:, 2, :].unsqueeze(2).to_broadcast([P, TT, H2]), ALU.mult).then_inc(awn_ready, 1)
                if c >= 1:
                    take_output(banks, turn, c - 1)
                if c >= 1:
                    dve.wait_ge(y_ready, turn * NC + (c - 1 + OPEN))
                for pair in range(2):
                    item = ("f", c, pair)
                    src = banks.arrived(item).rearrange("p (t d) -> p t d", t=2)
                    v.tensor_tensor(f2[p][:, 2 * pair:2 * pair + 2, :], src,
                                    row_bc[:, 1:2, :].to_broadcast([P, 2, D]), ALU.add).then_inc(banks.free(item), 1)
                dve.drain().then_inc(fb_ready, 1)
                if there(segment, c + 1):
                    norm_lo(banks, turn, c + 1)
                dve.wait_ge(v2_ready, turn * NC + (c + 1))
                for j in range(IT):
                    item = ("aw", c, j)
                    v.tensor_tensor(v2[:, j, :], v2[:, j, :], banks.arrived(item), ALU.mult)\
                        .then_inc(banks.free(item), 1)
                for j in range(IT):
                    banks.was_read(("aw", c, j))
                    start = 0.0 if c % NC == 0 else state[1 - p][:, j, CH - 1:CH]
                    v.tensor_tensor_scan(state[p][:, j, :], decay[:, j:j + 1].to_broadcast([P, CH]), v2[:, j, :],
                                         start, ALU.mult, ALU.add).then_inc(state_ready, 1)
                dve.wait_ge(gate2_ready, turn * NC + (c + 1))
                dve.wait_ge(qs_ready, turn * NC + (c + 1 + OPEN))
                v.scalar_tensor_tensor(o2[:, :, :].rearrange("p j t -> p (j t)"),
                                       gate2[:, :, :].rearrange("p j t -> p (j t)"), 1.0,
                                       o2[:, :, :].rearrange("p j t -> p (j t)"),
                                       ALU.add, ALU.add).then_inc(o2_full, 1)

            run_dense(dve, SEG3, step)
            output_norm()
            take_output(Banks(dve, ring3, "tail", TURNS), TURNS, NC - 1)
            output_norm()

        @block.gpsimd
        def _(pool):
            g_ = nc.gpsimd

            def difference(turn, c):
                pool.wait_ge(xnt_ready, turn * NC + (c + 1 + OPEN))
                if c:
                    pool.wait_ge(mix_ready, turn * NC + c)
                now, before = xn_t[c % 2][:, :, 1:CH + 1], xn_t[c % 2][:, :, 0:CH]
                g_.tensor_tensor(x_dif[:, :, :], now, before, ALU.subtract).then_inc(dif_ready, 1)

            difference(0, 0)
            pool.wait_ge(tables_in, 3 * 16)

            def step(segment, turn, c):
                banks = Banks(pool, ring1, segment, turn)

                def rotate(j):
                    banks.was_read(("qk", c, j))
                    g_.tensor_tensor(r_sin[j][:, :], r_sin[j][:, :], sin_t[:, c * CH:(c + 1) * CH], ALU.mult)
                    pool.drain()
                    g_.tensor_tensor(r_cos[j][:, :], r_cos[j][:, :], r_sin[j][:, :], ALU.add).then_inc(rot_ready, 1)

                def low(j):
                    pool.wait_ge(mid_ready, turn * (4 * NC) + (4 * c + j + 1))
                    g_.tensor_tensor(parts[j][:, 2, :], r_cos[j][:, :], parts[j][:, 1, :], ALU.subtract).then_inc(lo_ready, 1)

                pool.wait_ge(xn_ready, turn * NC + (c + 1))
                g_.tensor_tensor(x_in[c][:, :, :], x_in[c][:, :, :],
                                 b_out[:, :].unsqueeze(1).to_broadcast([P, TT, D]), ALU.add).then_inc(bias_added, 1)
                rotate(0)
                rotate(1)
                low(0)
                rotate(2)
                low(1)
                rotate(3)
                low(2)
                low(3)
                if there(segment, c + 1):
                    difference(turn, c + 1)

            run_dense(pool, SEG1, step)
            end_phase(pool, 1)

            for j in range(NSTK):
                g_.memset(k_stk[j][ROWS:ROWS + 2, :], 1.0)
            pool.drain().then_inc(ones_set, 1)
            for j in range(NSTK):
                g_.memset(v_head[j][:, :, HD:], 1.0)
            pool.drain().then_inc(ones_set, 1)

            def head(turn, j):
                pool.wait_ge(po_free[j % 3], turn + (j // 3 + OPEN))
                g_.tensor_copy(v_head[j % 3][:, :, 0:HD], v_all[:, bass.ds(turn * 3 + j, 1), :, :].squeeze(1)).then_inc(v_ready, 1)

            for n, name in enumerate(weight_shapes):
                pool.wait_ge(weight_hi, n + 1)
                g_.tensor_tensor(w_lo[name][:, :, :].bitcast(F32R), w_whole[name][:, :, :], w_hi[name][:, :, :],
                                 ALU.subtract).then_inc(weights_split, 1)

            run_heads(pool, head)
            end_phase(pool, 2)

            def attention_normal(turn, c):
                pool.wait_ge(heads_loaded[c % 2], turn * 128 + 64 * (c // 2 + 1))
                g_.tensor_tensor(a_raw[c % 2][:, :, :], a_raw[c % 2][:, :, :], a_sum[c % 2][:, :, :], ALU.mult)\
                    .then_inc(at_full, 1)

            def attention_lo(turn, c):
                pool.wait_ge(at_hi_ready, turn * NC + (c + 1))
                g_.tensor_tensor(a_lo[c % 2][:, :, :].bitcast(F32R), a_raw[c % 2][:, :, :], a_hi[c % 2][:, :, :],
                                 ALU.subtract).then_inc(at_ready, 1)

            def output_lo(turn, c):
                pool.wait_ge(o2_hi_ready, turn * NC + (c + 1))
                g_.tensor_tensor(o2_lo[:, :, :].bitcast(F32R), o2[:, :, :], o2_hi[:, :, :],
                                 ALU.subtract).then_inc(o2_ready, 1)

            def add_feed_forward(turn, c):
                pool.wait_ge(f2_ready, turn * NC + (c + 1))
                g_.tensor_tensor(xc[c % NC][:, :, :], xc[c % NC][:, :, :], f2[c % 2][:, :, :], ALU.add)

            def finish(turn, c):
                xp = xc[c % NC]
                pool.wait_ge(z2_ready, turn * NC + (c + 1))
                g_.tensor_tensor(z2[:, :, :], z2[:, :, :], row_bc[:, 2:3, :].to_broadcast([P, TT, D]), ALU.mult)
                pool.drain()
                g_.tensor_tensor(z2[:, :, :], z2[:, :, :], row_bc[:, 3:4, :].to_broadcast([P, TT, D]), ALU.add)
                pool.drain()
                g_.tensor_tensor(xp[:, :, :], xp[:, :, :], z2[:, :, :], ALU.add).then_inc(y_ready, 1)

            attention_normal(0, 0)
            attention_lo(0, 0)
            attention_normal(0, 1)
            attention_lo(0, 1)

            def step(segment, turn, c):
                if c >= 2:
                    finish(turn, c - 2)
                if there(segment, c + 2):
                    attention_normal(turn, c + 2)
                add_feed_forward(turn, c)
                for j in range(IT):
                    pool.wait_ge(state_ready, turn * (IT * NC) + (IT * c + j + 1))
                    last = g_.tensor_tensor(o2[:, j, :], q2[c % 2][:, j, :], state[c % 2][:, j, :], ALU.mult)
                last.then_inc(qs_ready, 1)
                if there(segment, c + 2):
                    attention_lo(turn, c + 2)
                output_lo(turn, c)

            run_dense(pool, SEG3, step)
            finish(TURNS, NC - 2)
            finish(TURNS, NC - 1)


def kernel(**inputs):
    import concourse.bacc as bacc
    from concourse.bass_utils import run_bass_kernel_spmd

    i = {k: np.asarray(x) for k, x in inputs.items()}
    order = np.concatenate([h * HD + np.concatenate([np.arange(0, HD, 2), np.arange(1, HD, 2)]) for h in range(H)])
    w = i["L0_attn_w_qkv"]

    def columns(*names):
        return np.stack([i[n].reshape(-1, P).T for n in names], axis=1)

    inv_freq = (1.0 / np.float32(10000.0) ** (np.arange(0, HD, 2, dtype=np.float32) / np.float32(HD))).astype(np.float32)
    angle = np.outer(np.arange(S, dtype=np.float32), inv_freq).astype(np.float32)
    row = np.arange(P) % HD
    cos = np.cos(angle).T[row % (HD // 2)]
    sin = np.sin(angle).T[row % (HD // 2)] * np.where(row < HD // 2, -1, 1)[:, None]
    arrays = {
        "x": i["L0_attn_x"],
        "w_qk": np.concatenate([w[0:D][order], w[D:2 * D][order]]).T,
        "w_v": w[2 * D:].T, "w_out": i["L0_attn_w_out"].T, "b_out": i["L0_attn_b_out"],
        "wf_r": i["L0_ffn_W_r"].T, "wf_k": i["L0_ffn_W_k"].T, "wf_v": i["L0_ffn_W_v"].T,
        "mu": columns("L0_ffn_mu_r", "L0_ffn_mu_k"),
        "cos": cos.astype(np.float32), "sin": sin.astype(np.float32), "ident": np.eye(P, dtype=np.float32),
        "w2_q": i["L1_attn_Wq"], "w2_k": i["L1_attn_Wk"], "w2_v": i["L1_attn_Wv"], "w_o2": i["L1_attn_Wo"],
        "col": columns("L1_attn_bq", "L1_attn_bk", "L1_attn_bv", "L1_attn_alpha", "L1_attn_aug_param"),
        "bo": i["L1_attn_bo"],
        "ln_scale": i["L1_attn_ln_scale"], "ln_bias": i["L1_attn_ln_bias"],
        "wa_w": i["L1_ffn_weight"].T, "wa_1": i["L1_ffn_aux_weight1"].T, "wa_2": i["L1_ffn_aux_weight2"],
        "f_bias": i["L1_ffn_bias"],
    }
    arrays = {k: np.ascontiguousarray(x) for k, x in arrays.items()}
    nc = bacc.Bacc("TRN2", target_bir_lowering=False, num_devices=1)
    aps = {k: nc.dram_tensor(f"in_{k}", x.shape, mybir.dt.from_np(x.dtype), kind="ExternalInput").ap()
           for k, x in arrays.items()}
    out = nc.dram_tensor("out_x", (B, S, D), F32, kind="ExternalOutput").ap()
    build(nc, aps, out)
    r = run_bass_kernel_spmd(nc, [{f"in_{k}": x for k, x in arrays.items()}], core_ids=[0])
    return r.results[0]["out_x"]
```
